# Optimizing a Trainium2 kernel written in Bass

```python
import numpy as np
import jax
import jax.numpy as jnp

def _softmax(x, axis=-1):
    return jax.nn.softmax(x, axis=axis)

def _gelu(x):
    return jax.nn.gelu(x, approximate=True)

def _silu(x):
    return jax.nn.silu(x)

def _sigmoid(x):
    return jax.nn.sigmoid(x)

def _layernorm(x, axis=-1, eps=1e-05):
    m = jnp.mean(x, axis=axis, keepdims=True)
    v = jnp.var(x, axis=axis, keepdims=True)
    return (x - m) / jnp.sqrt(v + eps)

def _scatter_add(tgt, idx, src, axis=0):
    return tgt.at[idx].add(src)

def _segment_sum(src, seg, n):
    return jax.ops.segment_sum(src, seg, n)
kernel_name = 'mk_xattn_seq_d2_seqx_r4_8443ef'

def setup_inputs(seed: int=0):
    np.random.seed(seed)
    _w = jnp.asarray

    def _rec_inputs():
        import jax
        import jax.numpy as jnp
        _rk = jax.random.key(seed)
        x = -0.0002928 + 1 * jax.random.normal(jax.random.fold_in(_rk, 1), (4, 512, 512), jnp.float32)
        _lenS = 512 - jax.random.randint(jax.random.fold_in(_rk, 7), (4,), 0, max(1, 512 // 4) + 1, jnp.int32)
        _lenS2 = 512 - jax.random.randint(jax.random.fold_in(_rk, 8), (4,), 0, max(1, 512 // 4) + 1, jnp.int32)
        _ctx_2048P = jax.random.normal(jax.random.fold_in(_rk, 11), (4, 16, 512), jnp.float32)
        _ctx_2048c = jax.random.dirichlet(jax.random.fold_in(_rk, 511), 0.3 * jnp.ones((16,), jnp.float32), (4, 512))
        _ctx_2048t = jnp.einsum('bsk,bkd->bsd', _ctx_2048c, _ctx_2048P)
        _ctx_2048t = _ctx_2048t * jax.lax.rsqrt(jnp.mean(jnp.square(_ctx_2048t)) + 1e-12) * 0.953939
        ctx_2048 = -1.39393e-06 + 0.999914 * (_ctx_2048t + 0.3 * jax.random.normal(jax.random.fold_in(_rk, 611), (4, 512, 512), jnp.float32))
        _validS = jnp.arange(512)[None, :] < _lenS[:, None]
        _validS2 = jnp.arange(512)[None, :] < _lenS2[:, None]
        _causal = jnp.tril(jnp.ones((512, 512), dtype=bool))
        mask_1x1xSxS2_fc1 = jnp.where(jnp.broadcast_to(_validS2[0:1, None, None, :], (1, 1, 512, 512)), 1.0, 0.0).astype(jnp.float32)
        mask_Bx1xSxS2_ff1 = jnp.where(jnp.ones((4, 1, 512, 512), dtype=bool), 1.0, 0.0).astype(jnp.float32)
        return (x, ctx_2048, mask_1x1xSxS2_fc1, mask_Bx1xSxS2_ff1)
    x, ctx_2048, mask_1x1xSxS2_fc1, mask_Bx1xSxS2_ff1 = _rec_inputs()

    def _L0_xattn_setup():
        import jax, jax.numpy as jnp
        import numpy as np
        H = 512
        NH = 16
        HD = H // NH
        EPS = 1e-05

        def gelu(x):
            return 0.5 * x * (1.0 + jnp.tanh(0.7978845608028654 * x * (1.0 + 0.044715 * x * x)))

        def layernorm(x, scale, bias):
            m = jnp.mean(x, axis=-1, keepdims=True)
            v = jnp.mean(jnp.square(x - m), axis=-1, keepdims=True)
            return (x - m) * jax.lax.rsqrt(v + EPS) * scale + bias

        def split_heads(x):
            b, s, _ = x.shape
            return x.reshape(b, s, NH, HD).transpose(0, 2, 1, 3)

        def merge_heads(x):
            b, nh, s, hd = x.shape
            return x.transpose(0, 2, 1, 3).reshape(b, s, nh * hd)

        def attention(q, k, v, mask):
            scores = jnp.einsum('bhqd,bhkd->bhqk', q, k) / jnp.sqrt(jnp.float32(HD))
            scores = scores * mask - 10000.0 * (1.0 - mask)
            probs = jax.nn.softmax(scores, axis=-1)
            return jnp.einsum('bhqk,bhkd->bhqd', probs, v)
        key = jax.random.key(seed)
        ks = jax.random.split(key, 16)
        b, s, t = (2, 256, 256)
        w = lambda k, i, o: jax.random.normal(k, (i, o), jnp.float32) * 0.02
        inp = {'hidden_states': jax.random.normal(ks[0], (b, s, H), jnp.float32), 'encoder_states': jax.random.normal(ks[1], (b, t, H), jnp.float32), 'ltor_mask': jnp.tril(jnp.ones((1, 1, s, s), jnp.float32)), 'cross_mask': jnp.ones((b, 1, s, t), jnp.float32), 'ln1_s': jnp.ones((H,), jnp.float32), 'ln1_b': jnp.zeros((H,), jnp.float32), 'w_qkv': w(ks[2], H, 3 * H), 'b_qkv': jnp.zeros((3 * H,), jnp.float32), 'w_ao': w(ks[3], H, H), 'b_ao': jnp.zeros((H,), jnp.float32), 'ln2_s': jnp.ones((H,), jnp.float32), 'ln2_b': jnp.zeros((H,), jnp.float32), 'w_q': w(ks[4], H, H), 'b_q': jnp.zeros((H,), jnp.float32), 'w_kv': w(ks[5], H, 2 * H), 'b_kv': jnp.zeros((2 * H,), jnp.float32), 'w_co': w(ks[6], H, H), 'b_co': jnp.zeros((H,), jnp.float32), 'ln3_s': jnp.ones((H,), jnp.float32), 'ln3_b': jnp.zeros((H,), jnp.float32), 'w1': w(ks[7], H, 4 * H), 'b1': jnp.zeros((4 * H,), jnp.float32), 'w2': w(ks[8], 4 * H, H), 'b2': jnp.zeros((H,), jnp.float32)}
        return inp
    _L0_xattn_all = _L0_xattn_setup()
    _L0_xattn_in = {k: v for k, v in _L0_xattn_all.items() if k in ('ln1_s', 'ln1_b', 'w_qkv', 'b_qkv', 'w_ao', 'b_ao', 'ln2_s', 'ln2_b', 'w_q', 'b_q', 'w_kv', 'b_kv', 'w_co', 'b_co', 'ln3_s', 'ln3_b', 'w1', 'b1', 'w2', 'b2')}
    del _L0_xattn_all

    def _L1_xattn_setup():
        import jax, jax.numpy as jnp
        import numpy as np
        H = 512
        B, L, S = (4, 1024, 10)
        key = jax.random.key(seed)
        k1, k2, k3, k4, k5, k6 = jax.random.split(key, 6)
        scale = 1.0 / np.sqrt(H)
        return {'h_english': jax.random.normal(k1, (B, L, H), dtype=jnp.float32), 'h_lojban': jax.random.normal(k2, (B, S, H), dtype=jnp.float32), 'w_q': jax.random.normal(k3, (H, H), dtype=jnp.float32) * scale, 'w_k': jax.random.normal(k4, (H, H), dtype=jnp.float32) * scale, 'w_v': jax.random.normal(k5, (H, H), dtype=jnp.float32) * scale, 'w_o': jax.random.normal(k6, (H, H), dtype=jnp.float32) * scale, 'alpha': jnp.float32(0.1)}
    _L1_xattn_all = _L1_xattn_setup()
    _L1_xattn_in = {k: v for k, v in _L1_xattn_all.items() if k in ('w_q', 'w_k', 'w_v', 'w_o', 'alpha')}
    del _L1_xattn_all
    return {'x': x, 'ctx_2048': ctx_2048, 'mask_1x1xSxS2_fc1': mask_1x1xSxS2_fc1, 'mask_Bx1xSxS2_ff1': mask_Bx1xSxS2_ff1, 'L0_xattn_ln1_s': _L0_xattn_in['ln1_s'], 'L0_xattn_ln1_b': _L0_xattn_in['ln1_b'], 'L0_xattn_w_qkv': _L0_xattn_in['w_qkv'], 'L0_xattn_b_qkv': _L0_xattn_in['b_qkv'], 'L0_xattn_w_ao': _L0_xattn_in['w_ao'], 'L0_xattn_b_ao': _L0_xattn_in['b_ao'], 'L0_xattn_ln2_s': _L0_xattn_in['ln2_s'], 'L0_xattn_ln2_b': _L0_xattn_in['ln2_b'], 'L0_xattn_w_q': _L0_xattn_in['w_q'], 'L0_xattn_b_q': _L0_xattn_in['b_q'], 'L0_xattn_w_kv': _L0_xattn_in['w_kv'], 'L0_xattn_b_kv': _L0_xattn_in['b_kv'], 'L0_xattn_w_co': _L0_xattn_in['w_co'], 'L0_xattn_b_co': _L0_xattn_in['b_co'], 'L0_xattn_ln3_s': _L0_xattn_in['ln3_s'], 'L0_xattn_ln3_b': _L0_xattn_in['ln3_b'], 'L0_xattn_w1': _L0_xattn_in['w1'], 'L0_xattn_b1': _L0_xattn_in['b1'], 'L0_xattn_w2': _L0_xattn_in['w2'], 'L0_xattn_b2': _L0_xattn_in['b2'], 'L1_xattn_w_q': _L1_xattn_in['w_q'], 'L1_xattn_w_k': _L1_xattn_in['w_k'], 'L1_xattn_w_v': _L1_xattn_in['w_v'], 'L1_xattn_w_o': _L1_xattn_in['w_o'], 'L1_xattn_alpha': _L1_xattn_in['alpha']}

def reference(x, ctx_2048, mask_1x1xSxS2_fc1, mask_Bx1xSxS2_ff1, L0_xattn_ln1_s, L0_xattn_ln1_b, L0_xattn_w_qkv, L0_xattn_b_qkv, L0_xattn_w_ao, L0_xattn_b_ao, L0_xattn_ln2_s, L0_xattn_ln2_b, L0_xattn_w_q, L0_xattn_b_q, L0_xattn_w_kv, L0_xattn_b_kv, L0_xattn_w_co, L0_xattn_b_co, L0_xattn_ln3_s, L0_xattn_ln3_b, L0_xattn_w1, L0_xattn_b1, L0_xattn_w2, L0_xattn_b2, L1_xattn_w_q, L1_xattn_w_k, L1_xattn_w_v, L1_xattn_w_o, L1_xattn_alpha):
    import jax
    import jax.numpy as jnp

    def _L0_xattn_ref(hidden_states, encoder_states, ltor_mask, cross_mask, ln1_s, ln1_b, w_qkv, b_qkv, w_ao, b_ao, ln2_s, ln2_b, w_q, b_q, w_kv, b_kv, w_co, b_co, ln3_s, ln3_b, w1, b1, w2, b2):
        import jax, jax.numpy as jnp
        import numpy as np
        H = 512
        NH = 16
        HD = H // NH
        EPS = 1e-05

        def gelu(x):
            return 0.5 * x * (1.0 + jnp.tanh(0.7978845608028654 * x * (1.0 + 0.044715 * x * x)))

        def layernorm(x, scale, bias):
            m = jnp.mean(x, axis=-1, keepdims=True)
            v = jnp.mean(jnp.square(x - m), axis=-1, keepdims=True)
            return (x - m) * jax.lax.rsqrt(v + EPS) * scale + bias

        def split_heads(x):
            b, s, _ = x.shape
            return x.reshape(b, s, NH, HD).transpose(0, 2, 1, 3)

        def merge_heads(x):
            b, nh, s, hd = x.shape
            return x.transpose(0, 2, 1, 3).reshape(b, s, nh * hd)

        def attention(q, k, v, mask):
            scores = jnp.einsum('bhqd,bhkd->bhqk', q, k) / jnp.sqrt(jnp.float32(HD))
            scores = scores * mask - 10000.0 * (1.0 - mask)
            probs = jax.nn.softmax(scores, axis=-1)
            return jnp.einsum('bhqk,bhkd->bhqd', probs, v)
        ln_out = layernorm(hidden_states, ln1_s, ln1_b)
        qkv = ln_out @ w_qkv + b_qkv
        q, k, v = jnp.split(qkv, 3, axis=-1)
        ctx = merge_heads(attention(split_heads(q), split_heads(k), split_heads(v), ltor_mask))
        attn_out = ctx @ w_ao + b_ao
        x = hidden_states + attn_out
        ln_out = layernorm(x, ln2_s, ln2_b)
        q = ln_out @ w_q + b_q
        kv = encoder_states @ w_kv + b_kv
        k, v = jnp.split(kv, 2, axis=-1)
        ctx = merge_heads(attention(split_heads(q), split_heads(k), split_heads(v), cross_mask))
        cross_out = ctx @ w_co + b_co
        x = x + cross_out
        ln_out = layernorm(x, ln3_s, ln3_b)
        mlp_out = gelu(ln_out @ w1 + b1) @ w2 + b2
        return x + mlp_out

    def _L1_xattn_ref(h_english, h_lojban, w_q, w_k, w_v, w_o, alpha):
        import jax, jax.numpy as jnp
        import numpy as np
        H = 512
        B, L, S = (4, 1024, 10)
        h = h_english.shape[-1]
        q = jnp.einsum('blh,oh->blo', h_english, w_q)
        k = jnp.einsum('bsh,oh->bso', h_lojban, w_k)
        v = jnp.einsum('bsh,oh->bso', h_lojban, w_v)
        scores = jnp.einsum('blh,bsh->bls', q, k) / jnp.sqrt(jnp.float32(h))
        probs = jax.nn.softmax(scores, axis=-1)
        context = jnp.einsum('bls,bsh->blh', probs, v)
        delta = jnp.einsum('blh,oh->blo', context, w_o)
        return h_english + alpha * delta
    x = _L0_xattn_ref(x, ctx_2048, mask_1x1xSxS2_fc1, mask_Bx1xSxS2_ff1, L0_xattn_ln1_s, L0_xattn_ln1_b, L0_xattn_w_qkv, L0_xattn_b_qkv, L0_xattn_w_ao, L0_xattn_b_ao, L0_xattn_ln2_s, L0_xattn_ln2_b, L0_xattn_w_q, L0_xattn_b_q, L0_xattn_w_kv, L0_xattn_b_kv, L0_xattn_w_co, L0_xattn_b_co, L0_xattn_ln3_s, L0_xattn_ln3_b, L0_xattn_w1, L0_xattn_b1, L0_xattn_w2, L0_xattn_b2)
    x = _L1_xattn_ref(x, ctx_2048, L1_xattn_w_q, L1_xattn_w_k, L1_xattn_w_v, L1_xattn_w_o, L1_xattn_alpha)
    return x

_drawn_inputs = setup_inputs


def setup_inputs(seed=0):
    import zlib

    import numpy as np

    out = dict(_drawn_inputs(seed))
    spreads = {'L0_xattn_ln1_s': (1.0, 0.6),
     'L0_xattn_ln1_b': (0.0, 0.405),
     'L0_xattn_b_qkv': (0.0, 0.1),
     'L0_xattn_b_ao': (0.0, 0.1),
     'L0_xattn_ln2_s': (1.0, 0.6),
     'L0_xattn_ln2_b': (0.0, 0.8),
     'L0_xattn_b_q': (0.0, 2.0),
     'L0_xattn_b_kv': (0.0, 0.1),
     'L0_xattn_b_co': (0.0, 0.1),
     'L0_xattn_ln3_s': (1.0, 0.2),
     'L0_xattn_ln3_b': (0.0, 0.326),
     'L0_xattn_b1': (0.0, 0.1),
     'L0_xattn_b2': (0.0, 0.1)}
    factors = {'L0_xattn_w_q': 7.444, 'L1_xattn_w_q': 2.968, 'L1_xattn_w_k': 2.963}
    for name, (base, spread) in spreads.items():
        noise = np.random.default_rng([zlib.crc32(name.encode()), seed]).standard_normal(out[name].shape)
        drawn = base * np.exp(spread * noise) if base else spread * noise
        out[name] = jnp.asarray(drawn.astype(out[name].dtype))
    for name, factor in factors.items():
        out[name] = (out[name] * factor).astype(out[name].dtype)
    return out
```

```python
from contextlib import ExitStack

import concourse.bass as bass
from concourse import mybir

F32 = mybir.dt.float32
F32R = mybir.dt.float32r
ALU = mybir.AluOpType
ACT = mybir.ActivationFunctionType

P = 128
B, S, H = 4, 512, 512
NH, HD = 16, 32
T = S // P
C = H // P
FF = 4 * H
M = FF // P
GH = P // HD
G = NH // GH
TILES = NH * T
EPS = 1e-5
HI, LO = 0, 1
PASSES = ((HI, HI), (LO, HI), (HI, LO))


def wait(eng, sem, value):
    if not isinstance(value, int) or value > 0:
        eng.wait_ge(sem, value)


def hold(dve, sem, value, cell):
    wait(dve, sem, value)
    dve.memset(cell, 0.0)


def over_batch(eng, step):
    step(0)
    with eng.Fori(1, B) as b:
        step(b)


class Place:

    def __init__(self, nc, ctx, phase):
        self.nc, self.ctx, self.phase, self.sems = nc, ctx, phase, []

    def sb(self, name, shape, dt=F32):
        return self.ctx.enter_context(self.nc.sbuf_tensor(f"{self.phase}_{name}", shape, dt))

    def sem(self, name):
        self.sems.append(self.ctx.enter_context(self.nc.semaphore(f"{self.phase}_{name}")))
        return self.sems[-1]

    def clear_sems(self):
        with self.nc.Block() as block:
            @block.sync
            def _(sp):
                for s in self.sems:
                    sp.sem_clear(s)


def chunks(w):
    return w.rearrange("(c p) n -> p c n", p=P)


def tiles(x, b):
    return x[b, :, :].rearrange("(t p) n -> p t n", p=P)


def row(v, n):
    return v.rearrange("(a n) -> a n", a=1).broadcast_to([P, n])


def project_phase(nc, name, ps, ident, x, norm, transposed, natural, scratch):
    blocks = [w for w, _, _ in transposed] + [w for w, _ in natural]
    nb, nt = len(blocks), len(transposed)
    outs = nb * G
    with ExitStack() as ctx, ExitStack() as work:
        pl = Place(nc, ctx, name)
        staged = pl.sb("staged", [P, nb, C, H])
        w = pl.sb("w", [P, nb, 2, C, H], F32R)
        xt = pl.sb("xt", [P, T, H])
        xh = pl.sb("xh", [P, T, H]) if norm else xt
        stats = pl.sb("stats", [P, T, 6])
        mv = pl.sb("mv", [P, T, 2])
        std = pl.sb("std", [P, T])
        rstd = pl.sb("rstd", [P, T])
        eps = pl.sb("eps", [P, 1])
        held = pl.sb("held", [P, 1])
        ln_s = pl.sb("ln_s", [P, C])
        ln_b = pl.sb("ln_b", [P, C])
        full = pl.sb("full", [P, 2, S])
        xT = pl.sb("xT", [P, 2, C, S], F32R)
        bcol = pl.sb("bcol", [P, max(nt, 1), G])
        brow = pl.sb("brow", [P, H])
        out = pl.sb("out", [P, 4, 2, S], F32R)

        w_in = pl.sem("w_in")
        w_hi = pl.sem("w_hi")
        w_lo = pl.sem("w_lo")
        x_in = pl.sem("x_in")
        eps_set = pl.sem("eps_set")
        stat = pl.sem("stat")
        std_done = pl.sem("std_done")
        normed = pl.sem("normed")
        turned = pl.sem("turned")
        full_done = pl.sem("full_done")
        hi_done = pl.sem("hi_done")
        cut = pl.sem("cut")
        made = pl.sem("made")
        rounded = pl.sem("rounded")
        ready = pl.sem("ready")
        stored = [pl.sem(f"stored{i}") for i in range(4)]

        turn_bank = lambda n: ps[:, n % 2, :]
        made_bank = lambda n: ps[:, 4 + n % 4, :]
        block = work.enter_context(nc.Block())

        @block.sync
        def _(sp):
            loads = [(staged[:, i], chunks(blocks[i])) for i in range(nb)]
            loads += [(bcol[:, i, :], bias) for i, (_, bias, _) in enumerate(transposed)]
            loads += [(brow[:], row(bias, H)) for _, bias in natural]
            if norm:
                loads += [(ln_s[:], norm[0]), (ln_b[:], norm[1])]
            sp.dma_start(xt[:], tiles(x, 0)).then_inc(x_in, 16)
            for to, src in loads:
                sp.dma_start(to, src).then_inc(w_in, 16)

            def step(b):
                if not isinstance(b, int):
                    if norm:
                        wait(sp, normed, b * T)
                    else:
                        wait(sp, turned, b * C)
                    sp.dma_start(xt[:], tiles(x, b)).then_inc(x_in, 16)
                for n in range(outs):
                    wait(sp, ready, b * outs + n + 1)
                    blk, g = divmod(n, G)
                    if blk < nt:
                        to = scratch["heads"][transposed[blk][2], b, g, :, :, :]
                        sp.dma_start(to.rearrange("k p n -> p k n"), out[:, n % 4].bitcast(F32))\
                          .then_inc(stored[n % 4], 16)
                    else:
                        sp.dma_start(scratch["v"][b, :, g, :], out[:, n % 4, 0, :].bitcast(F32))\
                          .then_inc(stored[n % 4], 16)

            over_batch(sp, step)
            for s in stored:
                sp.wait_ge(s, 16 * B * outs // 4)

        @block.scalar
        def _(act):
            n_in = 16 * (nb + nt + len(natural) + (2 if norm else 0))
            act.wait_ge(w_in, n_in)
            for i in range(nb):
                act.activation(w[:, i, HI], staged[:, i], ACT.Copy).then_inc(w_hi, 1)
            act.wait_ge(eps_set, 1)

            def step(b):
                if norm:
                    act.wait_ge(stat, b * (2 * T + 1) + 2 * T)
                    act.activation(std[:], mv[:, :, 1], ACT.Sqrt, bias=eps[:, 0:1]).then_inc(std_done, 1)
                for c in range(C):
                    n = b * C + c
                    wait(act, cut, n - 1)
                    act.wait_ge(turned, n + 1)
                    if norm:
                        act.activation(full[:, c % 2], turn_bank(c), ACT.Identity, bias=ln_b[:, c:c + 1],
                                       scale=ln_s[:, c:c + 1]).then_inc(full_done, 1)
                    else:
                        act.activation(full[:, c % 2], turn_bank(c), ACT.Copy).then_inc(full_done, 1)
                for n in range(nt * G):
                    blk, g = divmod(n, G)
                    use = b * (outs // 4) + n // 4
                    wait(act, stored[n % 4], 16 * use)
                    act.wait_ge(made, b * outs + n + 1)
                    act.activation(out[:, n % 4, HI], made_bank(n), ACT.Identity, bias=bcol[:, blk, g:g + 1])\
                       .then_inc(rounded, 1)

            over_batch(act, step)

        @block.vector
        def _(dve):
            dve.memset(eps[:], EPS).then_inc(eps_set, 1)
            dve.wait_ge(w_in, 16 * (nb + nt + len(natural) + (2 if norm else 0)))
            for i in range(nb):
                dve.wait_ge(w_hi, i + 1)
                dve.tensor_tensor(w[:, i, LO], staged[:, i], w[:, i, HI].bitcast(F32), ALU.subtract)\
                   .then_inc(w_lo, 1)

            def step(b):
                dve.wait_ge(x_in, 16 * b + 16)
                if norm:
                    done = b * (2 * T + 1)
                    for t in range(T):
                        dve.bn_stats(stats[:, t, :], xt[:, t, :]).then_inc(stat, 1)
                    hold(dve, stat, done + T, held[:, 0:1])
                    for t in range(T):
                        dve.bn_aggr(mv[:, t, :], stats[:, t, :]).then_inc(stat, 1)
                    dve.wait_ge(std_done, b + 1)
                    dve.reciprocal(rstd[:], std[:]).then_inc(stat, 1)
                    dve.wait_ge(stat, done + 2 * T + 1)
                    wait(dve, turned, b * C)
                    for t in range(T):
                        dve.tensor_scalar(xh[:, t, :], xt[:, t, :], mv[:, t, 0:1], rstd[:, t:t + 1],
                                          ALU.subtract, ALU.mult).then_inc(normed, 1)
                wait(dve, made, b * outs)
                for c in range(C):
                    n = b * C + c
                    dve.wait_ge(full_done, n + 1)
                    dve.tensor_copy(xT[:, HI, c], full[:, c % 2]).then_inc(hi_done, 1)
                    dve.wait_ge(hi_done, n + 1)
                    dve.tensor_tensor(xT[:, LO, c], full[:, c % 2], xT[:, HI, c].bitcast(F32), ALU.subtract)\
                       .then_inc(cut, 1)
                for n in range(outs):
                    blk, g = divmod(n, G)
                    use = b * (outs // 4) + n // 4
                    if blk < nt:
                        dve.wait_ge(rounded, b * nt * G + n + 1)
                        dve.scalar_tensor_tensor(out[:, n % 4, LO], made_bank(n), bcol[:, blk, g:g + 1],
                                                 out[:, n % 4, HI].bitcast(F32), ALU.add, ALU.subtract)\
                           .then_inc(ready, 1)
                    else:
                        wait(dve, stored[n % 4], 16 * use)
                        dve.wait_ge(made, b * outs + n + 1)
                        dve.tensor_tensor(out[:, n % 4, 0].bitcast(F32), made_bank(n), brow[:], ALU.add)\
                           .then_inc(ready, 1)

            over_batch(dve, step)

        @block.tensor
        def _(pe):
            def step(b):
                for c in range(C):
                    n = b * C + c
                    wait(pe, full_done, n - 1)
                    if c == 0:
                        if norm:
                            pe.wait_ge(normed, b * T + T)
                        else:
                            pe.wait_ge(x_in, 16 * b + 16)
                    for t in range(T):
                        mm = pe.transpose(turn_bank(c)[:, t * P:(t + 1) * P], xh[:, t, c * P:(c + 1) * P], ident[:])
                    mm.then_inc(turned, 1)
                pe.wait_ge(cut, b * C + C)
                pe.wait_ge(w_lo, nb)
                for n in range(outs):
                    blk, g = divmod(n, G)
                    wait(pe, ready, b * outs + n - 3)
                    k = 0
                    for c in range(C):
                        for a, m in PASSES:
                            part = slice(g * P, (g + 1) * P)
                            if blk < nt:
                                lhsT, rhs = w[:, blk, a, c, part], xT[:, m, c, :]
                            else:
                                lhsT, rhs = xT[:, a, c, part], w[:, blk, m, c, :]
                            mm = pe.matmul(made_bank(n), lhsT, rhs, start=(k == 0), stop=(k == 3 * C - 1))
                            k += 1
                    mm.then_inc(made, 1)

            over_batch(pe, step)

        work.close()
        pl.clear_sems()


def attention_phase(nc, name, ps, ident, scratch, q_slot, k_slot, mask, w_o, b_o, x, x_out):
    per_seq_mask = mask.shape[0] == B
    SLOTS = 8
    RING = 8
    BANKS = 3
    ADD_LAG = 1
    LAG = 4
    TAKE_LAG = LAG - 1
    with ExitStack() as ctx, ExitStack() as work:
        pl = Place(nc, ctx, name)
        qs = pl.sb("qs", [3 * HD, SLOTS, S], F32R)
        ks = pl.sb("ks", [3 * HD, SLOTS, S], F32R)
        v = pl.sb("v", [P, T, H])
        msk = pl.sb("msk", [P, T, S])
        away = pl.sb("away", [P, T, S])
        tile = pl.sb("tile", [P, RING, S])
        least = pl.sb("least", [P, RING])
        held = pl.sb("held", [P, 2])
        rowsum = pl.sb("rowsum", [P, 2, GH, T])
        inv = pl.sb("inv", [P, GH, T])
        spread = pl.sb("spread", [P, T, GH, HD])
        ones = pl.sb("ones", [P, GH, HD])
        scale = pl.sb("scale", [P, S])
        pT = pl.sb("pT", [P, 2, GH, T, S])
        cn = pl.sb("cn", [P, S])
        cT = pl.sb("cT", [P, 2, G, S], F32R)
        w = pl.sb("w", [P, 2, C, H], F32R)
        xt = pl.sb("xt", [P, T, H])
        brow = pl.sb("brow", [P, H])
        xo = pl.sb("xo", [P, 2, H])
        staged = pT[:, 0, :, 0, :]

        w_in, w_hi, w_lo = pl.sem("w_in"), pl.sem("w_hi"), pl.sem("w_lo")
        head_in = [pl.sem(f"head_in{i}") for i in range(SLOTS)]
        v_in, x_in = pl.sem("v_in"), pl.sem("x_in")
        mask_in = pl.sem("mask_in")
        away_done = pl.sem("away_done")
        scores = pl.sem("scores")
        masked = pl.sem("masked")
        added = pl.sem("added")
        probs = pl.sem("probs")
        turned = pl.sem("turned")
        taken = pl.sem("taken")
        ones_set = pl.sem("ones_set")
        inv_done = pl.sem("inv_done")
        spread_done = pl.sem("spread_done")
        scale_turned = pl.sem("scale_turned")
        scale_done = pl.sem("scale_done")
        ctx_made = pl.sem("ctx_made")
        ctx_done = pl.sem("ctx_done")
        ctx_hi, ctx_lo = pl.sem("ctx_hi"), pl.sem("ctx_lo")
        with_bias = pl.sem("with_bias")
        out_made = pl.sem("out_made")
        out_ready = pl.sem("out_ready")
        stored = [pl.sem(f"stored{i}") for i in range(2)]

        score_bank = lambda i: ps[:, i % BANKS, :]
        turn_bank = lambda i: ps[:, BANKS + i % BANKS, :]
        ctx_bank = ps[:, 6, :]
        out_bank = scale_bank = ps[:, 7, :]

        def last_user(i):
            return i - BANKS if i >= BANKS else max(k for k in range(-BANKS, 0) if (k + TILES) % BANKS == i)

        block = work.enter_context(nc.Block())

        def over_sequences(eng, step, late):
            step(0, None)
            with eng.Fori(1, B) as b:
                step(b, b - 1)
            for i in range(TILES):
                late(B - 1, i)

        PV_AT = LAG + 3
        OUT_AT = (14, 18, 22, 29)

        @block.sync
        def _(sp):
            sp.dma_start(staged, chunks(w_o)).then_inc(w_in, 16)
            sp.dma_start(brow[:], row(b_o, H)).then_inc(w_in, 16)
            if not per_seq_mask:
                sp.dma_start(msk[:], tiles(mask[:, 0], 0)).then_inc(mask_in, 16)

            def store(b):
                for t in range(T):
                    wait(sp, out_ready, b * T + t + 1)
                    sp.dma_start(x_out[b, t * P:(t + 1) * P, :], xo[:, t % 2, :]).then_inc(stored[t % 2], 16)

            def late(b, i):
                if i == 32:
                    store(b)

            def step(b, before):
                if per_seq_mask:
                    wait(sp, masked, b * TILES)
                    sp.dma_start(msk[:], tiles(mask[:, 0], b)).then_inc(mask_in, 16)
                for h in range(NH):
                    g, j = divmod(h, GH)
                    s, mine = h % SLOTS, slice(j * HD, (j + 1) * HD)
                    wait(sp, scores, b * TILES + (h - SLOTS + 1) * T)
                    q, k = (scratch["heads"][n, b, g, :, mine, :] for n in (q_slot, k_slot))
                    sp.dma_start(qs[0:2 * HD, s].bitcast(F32), q)\
                      .then_inc(head_in[s], 16)
                    sp.dma_start(qs[2 * HD:3 * HD, s].bitcast(F32), q[HI]).then_inc(head_in[s], 16)
                    sp.dma_start(ks[0:HD, s].bitcast(F32), k[HI]).then_inc(head_in[s], 16)
                    sp.dma_start(ks[HD:3 * HD, s].bitcast(F32), k).then_inc(head_in[s], 16)
                    if h == 4:
                        wait(sp, ctx_made, b * G)
                        sp.dma_start(v[:], scratch["v"][b, :, :, :]).then_inc(v_in, 16)
                    if before is not None and h == 8:
                        late(before, 32)
                    if h == 9:
                        wait(sp, out_ready, b * T)
                        sp.dma_start(xt[:], tiles(x, b)).then_inc(x_in, 16)

            over_sequences(sp, step, late)
            for s in stored:
                sp.wait_ge(s, 16 * B * T // 2)

        @block.gpsimd
        def _(pool):
            def spread_group(b, g):
                wait(pool, inv_done, b * G + g + 1)
                wait(pool, scale_turned, b * G + g)
                for t in range(T):
                    pool.tensor_tensor(spread[:, t], inv[:, :, t:t + 1].broadcast_to([P, GH, HD]), ones[:],
                                       ALU.mult).then_inc(spread_done, 1)

            def rest_of_group(b, g):
                wait(pool, ctx_hi, b * G + g + 1)
                pool.tensor_tensor(cT[:, LO, g], cn[:], cT[:, HI, g].bitcast(F32), ALU.subtract).then_inc(ctx_lo, 1)

            def late(b, i):
                if i == 4:
                    spread_group(b, G - 1)
                if i == 8:
                    rest_of_group(b, G - 1)

            def step(b, before):
                if before is not None:
                    late(before, 4)
                    late(before, 8)
                for g in range(G - 1):
                    spread_group(b, g)
                    rest_of_group(b, g)
                wait(pool, x_in, 16 * b + 16)
                for t in range(T):
                    pool.tensor_tensor(xt[:, t, :], xt[:, t, :], brow[:], ALU.add).then_inc(with_bias, 1)

            pool.memset(ones[:], 1.0).then_inc(ones_set, 1)
            pool.wait_ge(ones_set, 1)
            pool.wait_ge(w_in, 32)
            over_sequences(pool, step, late)

        @block.scalar
        def _(act):
            def end_group(b, g, i):
                if i == 9:
                    wait(act, scale_turned, b * G + g + 1)
                    wait(act, ctx_done, b * G + g)
                    act.activation(scale[:], scale_bank, ACT.Copy).then_inc(scale_done, 1)
                if i == 13:
                    wait(act, ctx_done, b * G + g + 1)
                    if g == 0:
                        wait(act, out_made, b * T)
                    act.activation(cT[:, HI, g], cn[:], ACT.Copy).then_inc(ctx_hi, 1)

            def take(b, n):
                h, t = divmod(n, T)
                g, j = divmod(h, GH)
                if n % (GH * T) == 0:
                    wait(act, ctx_made, b * G + g - 1)
                act.wait_ge(turned, b * TILES + n + 1)
                act.activation(pT[:, g % 2, j, :, t * P:(t + 1) * P],
                               turn_bank(n).rearrange("p (k q) -> p k q", k=T), ACT.Copy).then_inc(taken, 1)

            def late(b, i):
                if i < TAKE_LAG:
                    take(b, TILES - TAKE_LAG + i)
                if i < GH * T:
                    end_group(b, G - 1, i)

            def step(b, before):
                for i in range(TILES):
                    h, t = divmod(i, T)
                    g, j = divmod(h, GH)
                    if t == 0 and j == 0:
                        wait(act, inv_done, b * G + g - 1)
                    act.wait_ge(added, b * TILES + i + 1)
                    act.activation(tile[:, i % RING], tile[:, i % RING], ACT.Exp, scale=-1.0,
                                   bias=least[:, i % RING:i % RING + 1],
                                   accum_out=rowsum[:, g % 2, j, t:t + 1]).then_inc(probs, 1)
                    if before is not None:
                        late(before, i)
                    if i >= TAKE_LAG:
                        take(b, i - TAKE_LAG)
                    if g > 0:
                        end_group(b, g - 1, i % (GH * T))

            act.wait_ge(w_in, 32)
            act.activation(w[:, HI], staged, ACT.Copy).then_inc(w_hi, 1)
            act.wait_ge(w_lo, 1)
            over_sequences(act, step, late)

        @block.vector
        def _(dve):

            def add(b, n):
                t = n % T
                dve.tensor_tensor_reduce(out=tile[:, n % RING], in0=tile[:, n % RING], in1=away[:, t, :],
                                         scale=1.0, scalar=3.0e38, op0=ALU.add, op1=ALU.min,
                                         accum_out=least[:, n % RING:n % RING + 1]).then_inc(added, 1)

            def end_group(b, g, i):
                if i == 4:
                    wait(dve, probs, b * TILES + (g + 1) * GH * T)
                    wait(dve, spread_done, (b * G + g) * T)
                    dve.reciprocal(inv[:], rowsum[:, g % 2]).then_inc(inv_done, 1)
                if i == 12:
                    wait(dve, scale_done, b * G + g + 1)
                    wait(dve, ctx_made, b * G + g + 1)
                    wait(dve, ctx_lo, b * G + g)
                    dve.tensor_tensor(cn[:], ctx_bank, scale[:], ALU.mult).then_inc(ctx_done, 1)

            def out_tile(b, t):
                wait(dve, with_bias, b * T + t + 1)
                wait(dve, stored[t % 2], 16 * (b * (T // 2) + t // 2))
                wait(dve, out_made, b * T + t + 1)
                dve.tensor_tensor(xo[:, t % 2], out_bank, xt[:, t, :], ALU.add).then_inc(out_ready, 1)

            def late(b, i):
                if i < GH * T:
                    end_group(b, G - 1, i)
                if i - 1 in OUT_AT:
                    out_tile(b, OUT_AT.index(i - 1))

            def last_adds(b):
                hold(dve, masked, b * TILES + TILES, held[:, 0:1])
                for n in range(TILES - ADD_LAG, TILES):
                    add(b, n)

            def make_away(b):
                wait(dve, added, b * TILES)
                dve.wait_ge(mask_in, 16 * b + 16)
                dve.tensor_scalar(away[:], msk[:], -10000.0, 10000.0, ALU.mult, ALU.add).then_inc(away_done, 1)
                hold(dve, away_done, b + 1, held[:, 1:2])

            def step(b, before):
                if per_seq_mask or before is None:
                    if before is not None:
                        last_adds(before)
                    make_away(b)
                for i in range(TILES):
                    wait(dve, turned, b * TILES + i - RING + 1)
                    wait(dve, scores, b * TILES + i + 1)
                    wait(dve, masked, b * TILES + i - ADD_LAG + 1)
                    dve.scalar_tensor_tensor(tile[:, i % RING], score_bank(i), -float(HD) ** -0.5, msk[:, i % T, :],
                                             ALU.mult, ALU.mult).then_inc(masked, 1)
                    if i >= ADD_LAG:
                        add(b, i - ADD_LAG)
                    elif before is not None and not per_seq_mask:
                        add(before, TILES + i - ADD_LAG)
                    if before is not None:
                        late(before, i)
                    if i >= GH * T:
                        end_group(b, i // (GH * T) - 1, i % (GH * T))

            dve.wait_ge(w_hi, 1)
            dve.tensor_tensor(w[:, LO], staged, w[:, HI].bitcast(F32), ALU.subtract).then_inc(w_lo, 1)
            step(0, None)
            with dve.Fori(1, B) as b:
                step(b, b - 1)
            last_adds(B - 1)
            for i in range(TILES):
                late(B - 1, i)

        @block.tensor
        def _(pe):
            def turn(b, n):
                wait(pe, taken, b * TILES + last_user(n) + 1)
                wait(pe, probs, b * TILES + n + 1)
                for k in range(T):
                    mm = pe.transpose(turn_bank(n)[:, k * P:(k + 1) * P], tile[:, n % RING, k * P:(k + 1) * P], ident[:])
                mm.then_inc(turned, 1)

            def end_group(b, g, i):
                if i == 8:
                    wait(pe, spread_done, (b * G + g + 1) * T)
                    if g == 0:
                        wait(pe, out_ready, (b - 1) * T + T - 1)
                    for t in range(T):
                        mm = pe.transpose(scale_bank[:, t * P:(t + 1) * P],
                                          spread[:, t].rearrange("p j d -> p (j d)"), ident[:])
                    mm.then_inc(scale_turned, 1)
                if i == PV_AT:
                    if g == 0:
                        wait(pe, v_in, 16 * b + 16)
                    wait(pe, ctx_done, b * G + g)
                    wait(pe, taken, b * TILES + (g + 1) * GH * T)
                    for k in range(T):
                        for j in range(GH):
                            h = g * GH + j
                            mm = pe.matmul(ctx_bank[j * HD:(j + 1) * HD, :], v[:, k, h * HD:(h + 1) * HD],
                                           pT[:, g % 2, j, k, :], start=(k == 0), stop=(k == T - 1))
                    mm.then_inc(ctx_made, 1)

            def out_tile(b, t):
                wait(pe, ctx_lo, b * G + G)
                next_scale = t == T - 1 and not isinstance(b, int)
                wait(pe, scale_done, b * G + G + next_scale)
                wait(pe, out_ready, b * T + t)
                n = 0
                for c in range(C):
                    for a, m in PASSES:
                        mm = pe.matmul(out_bank, cT[:, a, c, t * P:(t + 1) * P], w[:, m, c, :],
                                       start=(n == 0), stop=(n == 3 * C - 1))
                        n += 1
                mm.then_inc(out_made, 1)

            def late(b, i):
                if i < LAG:
                    turn(b, TILES - LAG + i)
                if i < GH * T:
                    end_group(b, G - 1, i)
                if i in OUT_AT:
                    out_tile(b, OUT_AT.index(i))

            def step(b, before):
                for i in range(TILES):
                    h, t = divmod(i, T)
                    s = h % SLOTS
                    if t == 0:
                        use = b * (NH // SLOTS) + h // SLOTS + 1
                        pe.wait_ge(head_in[s], 64 * use)
                    wait(pe, masked, b * TILES + last_user(i) + 1)
                    pe.matmul(score_bank(i), qs[:, s, t * P:(t + 1) * P], ks[:, s, :], start=True, stop=True)\
                      .then_inc(scores, 1)
                    if before is not None:
                        late(before, i)
                    if i >= LAG:
                        turn(b, i - LAG)
                    if i >= GH * T:
                        end_group(b, i // (GH * T) - 1, i % (GH * T))

            over_sequences(pe, step, late)

        work.close()
        pl.clear_sems()


def mlp_phase(nc, name, ps, ident, x, norm, w1, b1, w2, b2, x_out):
    with ExitStack() as ctx, ExitStack() as work:
        pl = Place(nc, ctx, name)
        w1s = pl.sb("w1s", [P, 2, C, FF], F32R)
        w2s = pl.sb("w2s", [P, 2, M, H], F32R)
        staged = pl.sb("staged", [P, 2, FF])
        xt = pl.sb("xt", [P, T, H])
        stats = pl.sb("stats", [P, T, 6])
        mv = pl.sb("mv", [P, T, 2])
        std = pl.sb("std", [P, T])
        rstd = pl.sb("rstd", [P, T])
        eps = pl.sb("eps", [P, 1])
        held = pl.sb("held", [P, 1])
        ln_s = pl.sb("ln_s", [P, C])
        ln_b = pl.sb("ln_b", [P, C])
        b1c = pl.sb("b1c", [P, M])
        brow = pl.sb("brow", [P, H])
        xT = pl.sb("xT", [P, 2, C, S], F32R)
        gel = pl.sb("gel", [P, 2, S])
        hT = pl.sb("hT", [P, 2, 2, S], F32R)
        xo = pl.sb("xo", [P, 2, H])
        xh = staged[:, 0].rearrange("p (t n) -> p t n", t=T)
        full = staged[:, 1, 0:2 * S].rearrange("p (a n) -> p a n", a=2)

        par_in = pl.sem("par_in")
        staged_in = [pl.sem(f"staged_in{i}") for i in range(2)]
        w_hi, w_lo = pl.sem("w_hi"), pl.sem("w_lo")
        x_in, eps_set, stat, std_done = (pl.sem(n) for n in ("x_in", "eps_set", "stat", "std_done"))
        normed, turned, full_done, hi_done, cut = (pl.sem(n) for n in ("normed", "turned", "full_done", "hi_done", "cut"))
        hid_made = pl.sem("hid_made")
        gel_done = pl.sem("gel_done")
        gel_hi = pl.sem("gel_hi")
        gel_cut = pl.sem("gel_cut")
        hid_used = pl.sem("hid_used")
        with_bias = pl.sem("with_bias")
        out_ready = pl.sem("out_ready")
        stored = [pl.sem(f"stored{i}") for i in range(2)]

        turn_bank = lambda n: ps[:, n % 2, :]
        hid_bank = lambda n: ps[:, 2 + n % 2, :]
        out_bank = lambda t: ps[:, 4 + t, :]
        PIECES = 2 * C
        w1_piece = lambda n, part: w1s[:, part, n, :]
        w2_piece = lambda n, part: w2s[:, part, (n - C) * T:(n - C + 1) * T, :].rearrange("p m n -> p (m n)")
        piece = lambda n, part: w1_piece(n, part) if n < C else w2_piece(n, part)
        block = work.enter_context(nc.Block())

        @block.sync
        def _(sp):
            for n in range(PIECES):
                wait(sp, w_lo, n - 1)
                if n < C:
                    src = w1[n * P:(n + 1) * P, :]
                    to = staged[:, n % 2]
                else:
                    src = w2[(n - C) * FF // C:(n - C + 1) * FF // C, :].rearrange("(m p) n -> p m n", p=P)
                    to = staged[:, n % 2].rearrange("p (m n) -> p m n", n=H)
                sp.dma_start(to, src).then_inc(staged_in[n % 2], 16)
                if n == 0:
                    for to, src in ((ln_s[:], norm[0]), (ln_b[:], norm[1]),
                                    (b1c[:], b1), (brow[:], row(b2, H))):
                        sp.dma_start(to, src).then_inc(par_in, 16)

            def step(b):
                wait(sp, out_ready, b * T)
                sp.dma_start(xt[:], tiles(x, b)).then_inc(x_in, 16)
                for t in range(T):
                    sp.wait_ge(out_ready, b * T + t + 1)
                    sp.dma_start(x_out[b, t * P:(t + 1) * P, :], xo[:, t % 2, :]).then_inc(stored[t % 2], 16)

            over_batch(sp, step)
            for s in stored:
                sp.wait_ge(s, 16 * B * T // 2)

        @block.gpsimd
        def _(pool):
            def step(b):
                pool.wait_ge(normed, b * T + T)
                for t in range(T):
                    pool.tensor_tensor(xt[:, t, :], xt[:, t, :], brow[:], ALU.add).then_inc(with_bias, 1)

            pool.wait_ge(par_in, 64)
            over_batch(pool, step)

        @block.scalar
        def _(act):
            act.wait_ge(par_in, 64)
            act.wait_ge(eps_set, 1)
            for n in range(PIECES):
                act.wait_ge(staged_in[n % 2], 16 * (n // 2 + 1))
                act.activation(piece(n, HI), staged[:, n % 2], ACT.Copy).then_inc(w_hi, 1)
            act.wait_ge(w_lo, PIECES)

            def step(b):
                act.wait_ge(stat, b * (2 * T + 1) + 2 * T)
                act.activation(std[:], mv[:, :, 1], ACT.Sqrt, bias=eps[:, 0:1]).then_inc(std_done, 1)
                for c in range(C):
                    n = b * C + c
                    wait(act, cut, n - 1)
                    act.wait_ge(turned, n + 1)
                    act.activation(full[:, c % 2], turn_bank(c), ACT.Identity, bias=ln_b[:, c:c + 1],
                                   scale=ln_s[:, c:c + 1]).then_inc(full_done, 1)
                for m in range(M):
                    n = b * M + m
                    wait(act, gel_cut, n - 1)
                    act.wait_ge(hid_made, n + 1)
                    act.activation(gel[:, m % 2], hid_bank(m), ACT.Gelu_apprx_tanh, bias=b1c[:, m:m + 1])\
                       .then_inc(gel_done, 1)

            over_batch(act, step)

        @block.vector
        def _(dve):
            dve.memset(eps[:], EPS).then_inc(eps_set, 1)
            for n in range(PIECES):
                dve.wait_ge(w_hi, n + 1)
                dve.tensor_tensor(piece(n, LO), staged[:, n % 2], piece(n, HI).bitcast(F32), ALU.subtract)\
                   .then_inc(w_lo, 1)
            dve.wait_ge(w_lo, PIECES)

            def step(b):
                done = b * (2 * T + 1)
                dve.wait_ge(x_in, 16 * b + 16)
                for t in range(T):
                    dve.bn_stats(stats[:, t, :], xt[:, t, :]).then_inc(stat, 1)
                hold(dve, stat, done + T, held[:, 0:1])
                for t in range(T):
                    dve.bn_aggr(mv[:, t, :], stats[:, t, :]).then_inc(stat, 1)
                dve.wait_ge(std_done, b + 1)
                dve.reciprocal(rstd[:], std[:]).then_inc(stat, 1)
                dve.wait_ge(stat, done + 2 * T + 1)
                wait(dve, turned, b * C)
                for t in range(T):
                    dve.tensor_scalar(xh[:, t, :], xt[:, t, :], mv[:, t, 0:1], rstd[:, t:t + 1],
                                      ALU.subtract, ALU.mult).then_inc(normed, 1)
                wait(dve, hid_made, b * M)
                for c in range(C):
                    n = b * C + c
                    dve.wait_ge(full_done, n + 1)
                    dve.tensor_copy(xT[:, HI, c], full[:, c % 2]).then_inc(hi_done, 1)
                    dve.wait_ge(hi_done, n + 1)
                    dve.tensor_tensor(xT[:, LO, c], full[:, c % 2], xT[:, HI, c].bitcast(F32), ALU.subtract)\
                       .then_inc(cut, 1)
                for m in range(M):
                    n = b * M + m
                    wait(dve, hid_used, n - 1)
                    dve.wait_ge(gel_done, n + 1)
                    dve.tensor_copy(hT[:, m % 2, HI], gel[:, m % 2]).then_inc(gel_hi, 1)
                    dve.wait_ge(gel_hi, n + 1)
                    dve.tensor_tensor(hT[:, m % 2, LO], gel[:, m % 2], hT[:, m % 2, HI].bitcast(F32), ALU.subtract)\
                       .then_inc(gel_cut, 1)
                dve.wait_ge(with_bias, b * T + T)
                dve.wait_ge(hid_used, b * M + M)
                for t in range(T):
                    wait(dve, stored[t % 2], 16 * (b * (T // 2) + t // 2))
                    dve.tensor_tensor(xo[:, t % 2], out_bank(t), xt[:, t, :], ALU.add).then_inc(out_ready, 1)

            over_batch(dve, step)

        @block.tensor
        def _(pe):
            pe.wait_ge(w_lo, PIECES)

            def step(b):
                pe.wait_ge(normed, b * T + T)
                for c in range(C):
                    wait(pe, full_done, b * C + c - 1)
                    for t in range(T):
                        mm = pe.transpose(turn_bank(c)[:, t * P:(t + 1) * P], xh[:, t, c * P:(c + 1) * P], ident[:])
                    mm.then_inc(turned, 1)
                pe.wait_ge(cut, b * C + C)
                for m in range(M + 2):
                    if m < M:
                        wait(pe, gel_done, b * M + m - 1)
                        n = 0
                        for c in range(C):
                            for a, r in PASSES:
                                mm = pe.matmul(hid_bank(m), w1s[:, a, c, m * P:(m + 1) * P], xT[:, r, c, :],
                                               start=(n == 0), stop=(n == 3 * C - 1))
                                n += 1
                        mm.then_inc(hid_made, 1)
                    k = m - 2
                    if k >= 0:
                        if k == 0:
                            wait(pe, out_ready, b * T)
                        pe.wait_ge(gel_cut, b * M + k + 1)
                        for t in range(T):
                            for n, (a, r) in enumerate(PASSES):
                                mm = pe.matmul(out_bank(t), hT[:, k % 2, a, t * P:(t + 1) * P], w2s[:, r, k, :],
                                               start=(k == 0 and n == 0), stop=(k == M - 1 and n == 2))
                        mm.then_inc(hid_used, 1)

            over_batch(pe, step)

        work.close()
        pl.clear_sems()


def last_phase(nc, name, ps, ident, x, enc, w_q, w_k, w_v, w_o, alpha, x_out):
    with ExitStack() as ctx, ExitStack() as work:
        pl = Place(nc, ctx, name)
        ws = pl.sb("ws", [P, 4, C, H])
        woT = pl.sb("woT", [P, C, H])
        kq = pl.sb("kq", [P, 2, C, H], F32R)
        vo = pl.sb("vo", [P, 2, C, H], F32R)
        al = pl.sb("al", [P, 1])
        xt = pl.sb("xt", [P, 2, T, H])
        xT = pl.sb("xT", [P, 2, 2, C, S], F32R)
        gT = pl.sb("gT", [P, 2, C, S], F32R)
        u = pl.sb("u", [P, 2, T, H], F32R)
        sc = pl.sb("sc", [P, 4, S])
        least = pl.sb("least", [P, T])
        rowsum = pl.sb("rowsum", [P, T])
        inv = pl.sb("inv", [P, T])
        by = pl.sb("by", [P, T])
        pT = pl.sb("pT", [P, 2, 2, T, P], F32R)
        xo = pl.sb("xo", [P, 2, H])

        w_in = pl.sem("w_in")
        pre_made = pl.sem("pre_made")
        pre_hi = pl.sem("pre_hi")
        pre_done = pl.sem("pre_done")
        x_in, e_in = pl.sem("x_in"), pl.sem("e_in")
        turned = pl.sem("turned")
        turn_hi = pl.sem("turn_hi")
        cut = pl.sem("cut")
        made = pl.sem("made")
        made_hi = pl.sem("made_hi")
        made_cut = pl.sem("made_cut")
        scores = pl.sem("scores")
        least_done = pl.sem("least_done")
        probs = pl.sem("probs")
        inv_done, by_done = pl.sem("inv_done"), pl.sem("by_done")
        p_turned, p_hi, p_cut = pl.sem("p_turned"), pl.sem("p_hi"), pl.sem("p_cut")
        delta = pl.sem("delta")
        out_ready = pl.sem("out_ready")
        stored = [pl.sem(f"stored{i}") for i in range(2)]

        N_PRE = 3 * C
        bank2 = lambda n: ps[:, n % 2, :]
        bank4 = lambda n: ps[:, 4 + n % 4, :]
        score_bank = lambda t: ps[:, 2 + t % 2, :]
        block = work.enter_context(nc.Block())

        @block.sync
        def _(sp):
            for i, w in enumerate((w_q, w_k, w_v, w_o)):
                sp.dma_start(ws[:, i], chunks(w)).then_inc(w_in, 16)
            sp.dma_start(al[:], alpha.rearrange("(a n) -> a n", a=1).broadcast_to([P, 1])).then_inc(w_in, 16)

            def step(b):
                wait(sp, turned, b * 2 * C)
                sp.dma_start(xt[:, 1], tiles(enc, b)).then_inc(e_in, 16)
                wait(sp, out_ready, b * T)
                sp.dma_start(xt[:, 0], tiles(x, b)).then_inc(x_in, 16)
                for t in range(T):
                    sp.wait_ge(out_ready, b * T + t + 1)
                    sp.dma_start(x_out[b, t * P:(t + 1) * P, :], xo[:, t % 2, :]).then_inc(stored[t % 2], 16)

            over_batch(sp, step)
            for s in stored:
                sp.wait_ge(s, 16 * B * T // 2)

        @block.scalar
        def _(act):
            for n in range(N_PRE):
                i, c = divmod(n, C)
                act.wait_ge(pre_made, n + 1)
                to = woT[:, c, :] if i == 0 else (kq, vo)[i - 1][:, HI, c, :]
                act.activation(to, bank4(n), ACT.Copy).then_inc(pre_hi, 1)

            def step(b):
                for n in range(2 * C):
                    act.wait_ge(turned, b * 2 * C + n + 1)
                    if n == 0:
                        wait(act, scores, b * T)
                    act.activation(xT[:, 1 - n // C, HI, n % C], bank2(n), ACT.Copy).then_inc(turn_hi, 1)
                for n in range(2 * C):
                    act.wait_ge(made, b * 2 * C + n + 1)
                    if n == 0:
                        wait(act, delta, b * T)
                    to = gT[:, HI, n, :] if n < C else u[:, HI, n - C, :]
                    act.activation(to, bank4(n), ACT.Copy).then_inc(made_hi, 1)
                for t in range(T):
                    act.wait_ge(least_done, b * T + t + 1)
                    if t == 0:
                        wait(act, inv_done, b)
                    act.activation(sc[:, t], sc[:, t], ACT.Exp, scale=-1.0, bias=least[:, t:t + 1],
                                   accum_out=rowsum[:, t:t + 1]).then_inc(probs, 1)
                for t in range(T):
                    wait(act, delta, b * T + t - 1)
                    act.wait_ge(p_turned, b * T + t + 1)
                    act.activation(pT[:, t % 2, HI].rearrange("p k q -> p (k q)"), bank2(t), ACT.Copy)\
                       .then_inc(p_hi, 1)

            over_batch(act, step)

        @block.vector
        def _(dve):
            dve.wait_ge(w_in, 80)
            for n in range(C, N_PRE):
                i, c = divmod(n, C)
                dve.wait_ge(pre_hi, n + 1)
                w = (kq, vo)[i - 1]
                dve.tensor_tensor(w[:, LO, c, :], bank4(n), w[:, HI, c, :].bitcast(F32), ALU.subtract)\
                   .then_inc(pre_done, 1)

            def step(b):
                for n in range(2 * C):
                    which = 1 - n // C
                    dve.wait_ge(turn_hi, b * 2 * C + n + 1)
                    dve.tensor_tensor(xT[:, which, LO, n % C], bank2(n), xT[:, which, HI, n % C].bitcast(F32),
                                      ALU.subtract).then_inc(cut, 1)
                for n in range(2 * C):
                    dve.wait_ge(made_hi, b * 2 * C + n + 1)
                    to = gT[:, :, n, :] if n < C else u[:, :, n - C, :]
                    dve.tensor_tensor(to[:, LO], bank4(n), to[:, HI].bitcast(F32), ALU.subtract).then_inc(made_cut, 1)
                for t in range(T):
                    dve.wait_ge(scores, b * T + t + 1)
                    wait(dve, p_turned, b * T)
                    dve.tensor_scalar(sc[:, t], score_bank(t), -float(H) ** -0.5, None, ALU.mult, ALU.min,
                                      accum_out=least[:, t:t + 1]).then_inc(least_done, 1)
                dve.wait_ge(probs, b * T + T)
                dve.reciprocal(inv[:], rowsum[:]).then_inc(inv_done, 1)
                dve.wait_ge(inv_done, b + 1)
                dve.tensor_scalar(by[:], inv[:], al[:, 0:1], None, ALU.mult).then_inc(by_done, 1)
                for t in range(T + 1):
                    if t < T:
                        dve.wait_ge(p_hi, b * T + t + 1)
                        dve.tensor_tensor(pT[:, t % 2, LO].rearrange("p k q -> p (k q)"), bank2(t),
                                          pT[:, t % 2, HI].rearrange("p k q -> p (k q)").bitcast(F32),
                                          ALU.subtract).then_inc(p_cut, 1)
                    if t == 0:
                        dve.wait_ge(by_done, b + 1)
                    else:
                        k = t - 1
                        wait(dve, stored[k % 2], 16 * (b * (T // 2) + k // 2))
                        dve.wait_ge(delta, b * T + k + 1)
                        dve.scalar_tensor_tensor(xo[:, k % 2], bank4(k), by[:, k:k + 1], xt[:, 0, k, :],
                                                 ALU.mult, ALU.add).then_inc(out_ready, 1)

            over_batch(dve, step)

        @block.tensor
        def _(pe):
            pe.wait_ge(w_in, 80)
            for n in range(N_PRE):
                i, c = divmod(n, C)
                if C <= n - 4:
                    pe.wait_ge(pre_done, n - 4 - C + 1)
                elif n >= 4:
                    pe.wait_ge(pre_hi, n - 3)
                if i == 0:
                    for k in range(C):
                        mm = pe.transpose(bank4(n)[:, k * P:(k + 1) * P], ws[:, 3, k, c * P:(c + 1) * P], ident[:])
                else:
                    if i == 2 and c == 0:
                        pe.wait_ge(pre_hi, C)
                    for k in range(C):
                        if i == 1:
                            lhsT, rhs = ws[:, 1, k, c * P:(c + 1) * P], ws[:, 0, k, :]
                        else:
                            lhsT, rhs = ws[:, 2, k, c * P:(c + 1) * P], woT[:, k, :]
                        mm = pe.matmul(bank4(n), lhsT, rhs, start=(k == 0), stop=(k == C - 1))
                mm.then_inc(pre_made, 1)
            pe.wait_ge(pre_done, 2 * C)

            def product(bank, stationary, moving):
                n = 0
                for c in range(C):
                    for a, r in PASSES:
                        mm = pe.matmul(bank, stationary(a, c), moving(r, c), start=(n == 0), stop=(n == 3 * C - 1))
                        n += 1
                return mm

            def step(b):
                for n in range(2 * C):
                    which, c = 1 - n // C, n % C
                    if n == 0:
                        pe.wait_ge(e_in, 16 * b + 16)
                        wait(pe, p_cut, b * T)
                    if n == C:
                        pe.wait_ge(x_in, 16 * b + 16)
                    wait(pe, cut, b * 2 * C + n - 1)
                    for t in range(T):
                        mm = pe.transpose(bank2(n)[:, t * P:(t + 1) * P], xt[:, which, t, c * P:(c + 1) * P], ident[:])
                    mm.then_inc(turned, 1)
                pe.wait_ge(cut, b * 2 * C + 2 * C)
                for n in range(2 * C):
                    wait(pe, made_cut, b * 2 * C + n - 3)
                    wait(pe, out_ready, b * T)
                    part = slice((n % C) * P, (n % C + 1) * P)
                    if n < C:
                        mm = product(bank4(n), lambda a, c: kq[:, a, c, part], lambda r, c: xT[:, 1, r, c, :])
                    else:
                        mm = product(bank4(n), lambda a, c: xT[:, 1, a, c, part], lambda r, c: vo[:, r, c, :])
                    mm.then_inc(made, 1)
                for t in range(T):
                    pe.wait_ge(made_cut, b * 2 * C + C)
                    wait(pe, least_done, b * T + t - 1)
                    part = slice(t * P, (t + 1) * P)
                    product(score_bank(t), lambda a, c: xT[:, 0, a, c, part], lambda r, c: gT[:, r, c, :])\
                        .then_inc(scores, 1)
                pe.wait_ge(made_cut, b * 2 * C + 2 * C)

                def turn(t):
                    pe.wait_ge(probs, b * T + t + 1)
                    wait(pe, p_cut, b * T + t - 1)
                    for k in range(T):
                        mm = pe.transpose(bank2(t)[:, k * P:(k + 1) * P], sc[:, t, k * P:(k + 1) * P], ident[:])
                    mm.then_inc(p_turned, 1)

                turn(0)
                for t in range(T):
                    if t + 1 < T:
                        turn(t + 1)
                    pe.wait_ge(p_cut, b * T + t + 1)
                    product(bank4(t), lambda a, c: pT[:, t % 2, a, c, :], lambda r, c: u[:, r, c, :]).then_inc(delta, 1)

            over_batch(pe, step)


def layer_and_cross_attention_kernel(nc, a, out):
    with ExitStack() as ctx:
        scratch = {
            "heads": nc.dram_tensor("heads", [4, B, G, 2, P, S], F32, kind="Internal").ap(),
            "v": nc.dram_tensor("v_scratch", [B, P, T, H], F32, kind="Internal").ap(),
        }
        cross = {
            "heads": scratch["heads"],
            "v": nc.dram_tensor("cross_v_scratch", [B, P, T, H], F32, kind="Internal").ap(),
        }
        x1 = nc.dram_tensor("x1", [B, S, H], F32, kind="Internal").ap()
        x2 = nc.dram_tensor("x2", [B, S, H], F32, kind="Internal").ap()
        x3 = nc.dram_tensor("x3", [B, S, H], F32, kind="Internal").ap()
        ps = ctx.enter_context(nc.psum_tensor("ps", [P, 8, S], F32))
        ident = ctx.enter_context(nc.sbuf_tensor("ident", [P, P], F32))
        zeroed = ctx.enter_context(nc.semaphore("zeroed"))
        ident_set = ctx.enter_context(nc.semaphore("ident_set"))

        with nc.Block() as block:
            @block.gpsimd
            def _(pool):
                nc.gpsimd.memset(ident[:], 0.0).then_inc(zeroed, 1)
                pool.wait_ge(zeroed, 1)
                nc.gpsimd.affine_select(out=ident[:], in_=ident[:], compare_op=ALU.not_equal, fill=1.0, base=0,
                                        pattern=[[-1, P]], channel_multiplier=1).then_inc(ident_set, 1)
                pool.wait_ge(ident_set, 1)

        cqkv, ckv = a["columns_L0_xattn_b_qkv"], a["columns_L0_xattn_b_kv"]
        col = lambda v, i: v[:, i * C:(i + 1) * C]
        wqkv, wkv = a["L0_xattn_w_qkv"], a["L0_xattn_w_kv"]
        bqkv, bkv = a["L0_xattn_b_qkv"], a["L0_xattn_b_kv"]
        cut = lambda w, i: w[:, i * H:(i + 1) * H]
        vec = lambda v, i: v[i * H:(i + 1) * H]
        project_phase(nc, "self_qkv", ps, ident, a["x"], (a["columns_L0_xattn_ln1_s"], a["columns_L0_xattn_ln1_b"]),
                      [(cut(wqkv, 0), col(cqkv, 0), 0), (cut(wqkv, 1), col(cqkv, 1), 1)],
                      [(cut(wqkv, 2), vec(bqkv, 2))], scratch)
        project_phase(nc, "cross_kv", ps, ident, a["ctx_2048"], None,
                      [(cut(wkv, 0), col(ckv, 0), 3)], [(cut(wkv, 1), vec(bkv, 1))], cross)
        attention_phase(nc, "self_att", ps, ident, scratch, 0, 1, a["mask_1x1xSxS2_fc1"], a["L0_xattn_w_ao"],
                        a["L0_xattn_b_ao"], a["x"], x1)
        project_phase(nc, "cross_q", ps, ident, x1, (a["columns_L0_xattn_ln2_s"], a["columns_L0_xattn_ln2_b"]),
                      [(a["L0_xattn_w_q"], a["columns_L0_xattn_b_q"], 2)], [], cross)
        attention_phase(nc, "cross_att", ps, ident, cross, 2, 3, a["mask_Bx1xSxS2_ff1"], a["L0_xattn_w_co"],
                        a["L0_xattn_b_co"], x1, x2)
        mlp_phase(nc, "mlp", ps, ident, x2, (a["columns_L0_xattn_ln3_s"], a["columns_L0_xattn_ln3_b"]), a["L0_xattn_w1"],
                  a["columns_L0_xattn_b1"], a["L0_xattn_w2"], a["L0_xattn_b2"], x3)
        last_phase(nc, "last", ps, ident, x3, a["ctx_2048"], a["L1_xattn_w_q"], a["L1_xattn_w_k"],
                   a["L1_xattn_w_v"], a["L1_xattn_w_o"], a["L1_xattn_alpha"], out)


_INS = ["x", "ctx_2048", "mask_1x1xSxS2_fc1", "mask_Bx1xSxS2_ff1", "L0_xattn_ln1_s", "L0_xattn_ln1_b",
        "L0_xattn_w_qkv", "L0_xattn_b_qkv", "L0_xattn_w_ao", "L0_xattn_b_ao", "L0_xattn_ln2_s", "L0_xattn_ln2_b",
        "L0_xattn_w_q", "L0_xattn_b_q", "L0_xattn_w_kv", "L0_xattn_b_kv", "L0_xattn_w_co", "L0_xattn_b_co",
        "L0_xattn_ln3_s", "L0_xattn_ln3_b", "L0_xattn_w1", "L0_xattn_b1", "L0_xattn_w2", "L0_xattn_b2",
        "L1_xattn_w_q", "L1_xattn_w_k", "L1_xattn_w_v", "L1_xattn_w_o", "L1_xattn_alpha"]

_COLUMNS = ["L0_xattn_ln1_s", "L0_xattn_ln1_b", "L0_xattn_b_qkv", "L0_xattn_ln2_s", "L0_xattn_ln2_b",
            "L0_xattn_b_q", "L0_xattn_b_kv", "L0_xattn_ln3_s", "L0_xattn_ln3_b", "L0_xattn_b1"]


def kernel(**inputs):
    import numpy as _np
    import concourse.bacc as _bacc
    from concourse import mybir as _mybir
    from concourse.bass_utils import run_bass_kernel_spmd as _run

    nc = _bacc.Bacc("TRN2", target_bir_lowering=False, num_devices=1)
    arrays, args = {}, {}
    given = {name: _np.asarray(inputs[name]).reshape(inputs[name].shape or (1,)) for name in _INS}
    given |= {f"columns_{name}": given[name].reshape(-1, P).T for name in _COLUMNS}
    for name, a in given.items():
        a = _np.ascontiguousarray(a)
        arrays[f"in_{name}"] = a
        args[name] = nc.dram_tensor(f"in_{name}", a.shape, _mybir.dt.from_np(a.dtype), kind="ExternalInput").ap()
    out = nc.dram_tensor("out_0", (B, S, H), F32, kind="ExternalOutput").ap()
    layer_and_cross_attention_kernel(nc, args, out)
    r = _run(nc, [arrays], core_ids=[0])
    return r.results[0]["out_0"]
```

```python
from contextlib import ExitStack

import concourse.bass as bass
from concourse import mybir

F32 = mybir.dt.float32
F32R = mybir.dt.float32r
ALU = mybir.AluOpType
ACT = mybir.ActivationFunctionType

P = 128
B, S, H = 4, 512, 512
NH, HD = 16, 32
T = S // P
C = H // P
FF = 4 * H
M = FF // P
GH = P // HD
G = NH // GH
TILES = NH * T
EPS = 1e-5
HI, LO = 0, 1
PASSES = ((HI, HI), (LO, HI), (HI, LO))


def wait(eng, sem, value):
    if not isinstance(value, int) or value > 0:
        eng.wait_ge(sem, value)


def hold(dve, sem, value, cell):
    wait(dve, sem, value)
    dve.memset(cell, 0.0)


def over_batch(eng, step):
    step(0)
    with eng.Fori(1, B) as b:
        step(b)


class Place:

    def __init__(self, nc, ctx, phase):
        self.nc, self.ctx, self.phase, self.sems = nc, ctx, phase, []

    def sb(self, name, shape, dt=F32):
        return self.ctx.enter_context(self.nc.sbuf_tensor(f"{self.phase}_{name}", shape, dt))

    def sem(self, name):
        self.sems.append(self.ctx.enter_context(self.nc.semaphore(f"{self.phase}_{name}")))
        return self.sems[-1]

    def clear_sems(self):
        with self.nc.Block() as block:
            @block.sync
            def _(sp):
                for s in self.sems:
                    sp.sem_clear(s)


def chunks(w):
    return w.rearrange("(c p) n -> p c n", p=P)


def tiles(x, b):
    return x[b, :, :].rearrange("(t p) n -> p t n", p=P)


def row(v, n):
    return v.rearrange("(a n) -> a n", a=1).broadcast_to([P, n])


def project_phase(nc, name, ps, ident, x_in, x, norm, transposed, natural, scratch):
    blocks = [w for w, _, _ in transposed] + [w for w, _ in natural]
    nb, nt = len(blocks), len(transposed)
    outs = nb * G
    STATS = 2 * T + 1
    with ExitStack() as ctx, ExitStack() as work:
        pl = Place(nc, ctx, name)
        staged = pl.sb("staged", [P, nb, C, H])
        w = pl.sb("w", [P, nb, 2, C, H], F32R)
        xt = pl.sb("xt", [P, T, H])
        xh = pl.sb("xh", [P, T, H]) if norm else xt
        stats = pl.sb("stats", [P, T, 6])
        mv = pl.sb("mv", [P, T, 2])
        std = pl.sb("std", [P, T])
        rstd = pl.sb("rstd", [P, T])
        eps = pl.sb("eps", [P, 1])
        held = pl.sb("held", [P, 1])
        ln_s = pl.sb("ln_s", [P, C])
        ln_b = pl.sb("ln_b", [P, C])
        full = pl.sb("full", [P, C, S])
        xT = pl.sb("xT", [P, 2, C, S], F32R)
        bcol = pl.sb("bcol", [P, max(nt, 1), G])
        brow = pl.sb("brow", [P, H])
        out = pl.sb("out", [P, 4, 2, S], F32R)

        ln_in = pl.sem("ln_in")
        bias_in = pl.sem("bias_in")
        w_in = [pl.sem(f"w_in{i}") for i in range(nb)]
        w_hi = pl.sem("w_hi")
        w_lo = pl.sem("w_lo")
        eps_set = pl.sem("eps_set")
        stat = pl.sem("stat")
        std_done = pl.sem("std_done")
        normed = pl.sem("normed")
        turned = pl.sem("turned")
        full_done = pl.sem("full_done")
        hi_done = pl.sem("hi_done")
        cut = pl.sem("cut")
        chunk_free = pl.sem("chunk_free")
        made = pl.sem("made")
        rounded = pl.sem("rounded")
        ready = pl.sem("ready")
        stored = [pl.sem(f"stored{i}") for i in range(4)]

        turn_bank = lambda n: ps[:, n % 4, :]
        made_bank = lambda n: ps[:, 4 + n % 4, :]
        TURN_AT = [min(outs - 1, outs // 2 + c) for c in range(C)]
        block = work.enter_context(nc.Block())

        def over_ahead(eng, step):
            step(0, 1)
            with eng.Fori(1, B - 1) as b:
                step(b, b + 1)
            step(B - 1, None)

        @block.sync
        def _(sp):
            if norm:
                sp.dma_start(ln_s[:], norm[0]).then_inc(ln_in, 16)
                sp.dma_start(ln_b[:], norm[1]).then_inc(ln_in, 16)
            for i in range(nb):
                sp.dma_start(staged[:, i], chunks(blocks[i])).then_inc(w_in[i], 16)
                if i < nt:
                    sp.dma_start(bcol[:, i, :], transposed[i][1]).then_inc(bias_in, 16)
                else:
                    sp.dma_start(brow[:], row(natural[i - nt][1], H)).then_inc(bias_in, 16)

            def step(b):
                for n in range(outs):
                    wait(sp, ready, b * outs + n + 1)
                    blk, g = divmod(n, G)
                    if blk < nt:
                        to = scratch["heads"][transposed[blk][2], b, g, :, :, :]
                        sp.dma_start(to.rearrange("k p n -> p k n"), out[:, n % 4].bitcast(F32))\
                          .then_inc(stored[n % 4], 16)
                    else:
                        sp.dma_start(scratch["v"][b, :, g, :], out[:, n % 4, 0, :].bitcast(F32))\
                          .then_inc(stored[n % 4], 16)

            over_batch(sp, step)
            for s in stored:
                sp.wait_ge(s, 16 * B * outs // 4)

        @block.gpsimd
        def _(pool):
            pool.dma_start(xt[:], tiles(x, 0)).then_inc(x_in, 16)
            with pool.Fori(1, B) as b:
                if norm:
                    pool.wait_ge(normed, b * T)
                else:
                    pool.wait_ge(turned, b * C)
                pool.dma_start(xt[:], tiles(x, b)).then_inc(x_in, 16)

        @block.scalar
        def _(act):
            def root(b):
                if norm:
                    act.wait_ge(stat, b * STATS + 2 * T)
                    act.activation(std[:], mv[:, :, 1], ACT.Sqrt, bias=eps[:, 0:1]).then_inc(std_done, 1)

            def take(b, c):
                wait(act, cut, (b - 1) * C + c + 1)
                act.wait_ge(turned, b * C + c + 1)
                if norm:
                    act.activation(full[:, c], turn_bank(c), ACT.Identity, bias=ln_b[:, c:c + 1],
                                   scale=ln_s[:, c:c + 1]).then_inc(full_done, 1)
                else:
                    act.activation(full[:, c], turn_bank(c), ACT.Copy).then_inc(full_done, 1)

            def round_chunk(b, c):
                act.wait_ge(full_done, b * C + c + 1)
                if c < C - 1:
                    wait(act, chunk_free, (b - 1) * (C - 1) + c + 1)
                else:
                    wait(act, made, b * outs)
                act.activation(xT[:, HI, c], full[:, c], ACT.Copy).then_inc(hi_done, 1)

            def step(b, ahead):
                for n in range(outs):
                    blk, g = divmod(n, G)
                    if n == outs - 1 and ahead is not None:
                        for c in range(C):
                            if TURN_AT[c] >= n - 1:
                                take(ahead, c)
                        for c in range(C):
                            round_chunk(ahead, c)
                    if blk < nt:
                        wait(act, stored[n % 4], 16 * (b * (outs // 4) + n // 4))
                        act.wait_ge(made, b * outs + n + 1)
                        act.activation(out[:, n % 4, HI], made_bank(n), ACT.Identity, bias=bcol[:, blk, g:g + 1])\
                           .then_inc(rounded, 1)
                    if n == 0 and ahead is not None:
                        root(ahead)
                    if n < outs - 1 and ahead is not None:
                        for c in range(C):
                            if TURN_AT[c] + 1 == n:
                                take(ahead, c)

            act.wait_ge(eps_set, 1)
            if norm:
                act.wait_ge(ln_in, 32)
            root(0)
            for c in range(C):
                take(0, c)
            for c in range(C):
                round_chunk(0, c)
            for i in range(nb):
                act.wait_ge(w_in[i], 16)
                act.activation(w[:, i, HI], staged[:, i], ACT.Copy).then_inc(w_hi, 1)
            act.wait_ge(bias_in, 16 * nb)
            over_ahead(act, step)

        @block.vector
        def _(dve):
            def statistics(b):
                if norm:
                    dve.wait_ge(x_in, 16 * b + 16)
                    for t in range(T):
                        dve.bn_stats(stats[:, t, :], xt[:, t, :]).then_inc(stat, 1)
                    hold(dve, stat, b * STATS + T, held[:, 0:1])
                    for t in range(T):
                        dve.bn_aggr(mv[:, t, :], stats[:, t, :]).then_inc(stat, 1)

            def normalise(b):
                if norm:
                    dve.wait_ge(std_done, b + 1)
                    dve.reciprocal(rstd[:], std[:]).then_inc(stat, 1)
                    dve.wait_ge(stat, b * STATS + STATS)
                    wait(dve, turned, b * C)
                    for t in range(T):
                        dve.tensor_scalar(xh[:, t, :], xt[:, t, :], mv[:, t, 0:1], rstd[:, t:t + 1],
                                          ALU.subtract, ALU.mult).then_inc(normed, 1)

            def rest_of_chunk(b, c):
                dve.wait_ge(hi_done, b * C + c + 1)
                dve.tensor_tensor(xT[:, LO, c], full[:, c], xT[:, HI, c].bitcast(F32), ALU.subtract)\
                   .then_inc(cut, 1)

            def step(b, ahead):
                for n in range(outs):
                    blk, g = divmod(n, G)
                    if n == outs - 1 and ahead is not None:
                        for c in range(C):
                            rest_of_chunk(ahead, c)
                    if blk < nt:
                        dve.wait_ge(rounded, b * nt * G + n + 1)
                        dve.scalar_tensor_tensor(out[:, n % 4, LO], made_bank(n), bcol[:, blk, g:g + 1],
                                                 out[:, n % 4, HI].bitcast(F32), ALU.add, ALU.subtract)\
                           .then_inc(ready, 1)
                    else:
                        wait(dve, stored[n % 4], 16 * (b * (outs // 4) + n // 4))
                        dve.wait_ge(made, b * outs + n + 1)
                        dve.tensor_tensor(out[:, n % 4, 0].bitcast(F32), made_bank(n), brow[:], ALU.add)\
                           .then_inc(ready, 1)
                    if n == 0 and ahead is not None:
                        statistics(ahead)
                    if n == 1 and ahead is not None:
                        normalise(ahead)

            dve.memset(eps[:], EPS).then_inc(eps_set, 1)
            statistics(0)
            normalise(0)
            for c in range(C):
                rest_of_chunk(0, c)
            for i in range(nb):
                dve.wait_ge(w_hi, i + 1)
                dve.tensor_tensor(w[:, i, LO], staged[:, i], w[:, i, HI].bitcast(F32), ALU.subtract)\
                   .then_inc(w_lo, 1)
            dve.wait_ge(bias_in, 16 * nb)
            over_ahead(dve, step)

        @block.tensor
        def _(pe):
            def turn(b, c):
                wait(pe, full_done, (b - 1) * C + c + 1)
                if c == 0:
                    if norm:
                        pe.wait_ge(normed, b * T + T)
                    else:
                        pe.wait_ge(x_in, 16 * b + 16)
                for t in range(T):
                    mm = pe.transpose(turn_bank(c)[:, t * P:(t + 1) * P], xh[:, t, c * P:(c + 1) * P], ident[:])
                mm.then_inc(turned, 1)

            def step(b, ahead):
                for n in range(outs):
                    blk, g = divmod(n, G)
                    part = slice(g * P, (g + 1) * P)
                    if isinstance(b, int) and b == 0 and g == 0:
                        pe.wait_ge(w_lo, blk + 1)
                    wait(pe, ready, b * outs + n - 3)
                    for c in range(C):
                        if n == 0:
                            pe.wait_ge(cut, b * C + c + 1)
                        for k, (a, m) in enumerate(PASSES):
                            if blk < nt:
                                lhsT, rhs = w[:, blk, a, c, part], xT[:, m, c, :]
                            else:
                                lhsT, rhs = xT[:, a, c, part], w[:, blk, m, c, :]
                            mm = pe.matmul(made_bank(n), lhsT, rhs, start=(c == 0 and k == 0),
                                           stop=(c == C - 1 and k == 2))
                        if c == C - 1:
                            mm.then_inc(made, 1)
                        elif n == outs - 1:
                            mm.then_inc(chunk_free, 1)
                    if ahead is not None:
                        for c in range(C):
                            if TURN_AT[c] == n:
                                turn(ahead, c)

            for c in range(C):
                turn(0, c)
            over_ahead(pe, step)

        work.close()
        pl.clear_sems()


def attention_phase(nc, name, ps, ident, scratch, q_slot, k_slot, mask, w_o, b_o, x, x_out):
    per_seq_mask = mask.shape[0] == B
    SLOTS = 8
    RING = 8
    BANKS = 3
    ADD_LAG = 1
    LAG = 4
    TAKE_LAG = LAG - 1
    with ExitStack() as ctx, ExitStack() as work:
        pl = Place(nc, ctx, name)
        qs = pl.sb("qs", [3 * HD, SLOTS, S], F32R)
        ks = pl.sb("ks", [3 * HD, SLOTS, S], F32R)
        v = pl.sb("v", [P, T, H])
        msk = pl.sb("msk", [P, T, S])
        away = pl.sb("away", [P, T, S])
        tile = pl.sb("tile", [P, RING, S])
        least = pl.sb("least", [P, RING])
        held = pl.sb("held", [P, 2])
        rowsum = pl.sb("rowsum", [P, 2, GH, T])
        inv = pl.sb("inv", [P, GH, T])
        spread = pl.sb("spread", [P, T, GH, HD])
        ones = pl.sb("ones", [P, GH, HD])
        scale = pl.sb("scale", [P, S])
        pT = pl.sb("pT", [P, 2, GH, T, S])
        cn = pl.sb("cn", [P, S])
        cT = pl.sb("cT", [P, 2, G, S], F32R)
        w = pl.sb("w", [P, 2, C, H], F32R)
        xt = pl.sb("xt", [P, T, H])
        brow = pl.sb("brow", [P, H])
        xo = pl.sb("xo", [P, 2, H])
        staged = pT[:, 0, :, 0, :]

        w_in, w_hi, w_lo = pl.sem("w_in"), pl.sem("w_hi"), pl.sem("w_lo")
        head_in = [pl.sem(f"head_in{i}") for i in range(SLOTS)]
        v_in, x_in = pl.sem("v_in"), pl.sem("x_in")
        mask_in = [pl.sem(f"mask_in{t}") for t in range(T)]
        away_done = pl.sem("away_done")
        scores = pl.sem("scores")
        masked = pl.sem("masked")
        added = pl.sem("added")
        probs = pl.sem("probs")
        turned = pl.sem("turned")
        taken = pl.sem("taken")
        ones_set = pl.sem("ones_set")
        inv_done = pl.sem("inv_done")
        spread_done = pl.sem("spread_done")
        scale_turned = pl.sem("scale_turned")
        scale_done = pl.sem("scale_done")
        ctx_made = pl.sem("ctx_made")
        ctx_done = pl.sem("ctx_done")
        ctx_hi, ctx_lo = pl.sem("ctx_hi"), pl.sem("ctx_lo")
        with_bias = pl.sem("with_bias")
        out_made = pl.sem("out_made")
        out_ready = pl.sem("out_ready")
        stored = [pl.sem(f"stored{i}") for i in range(2)]

        score_bank = lambda i: ps[:, i % BANKS, :]
        turn_bank = lambda i: ps[:, BANKS + i % BANKS, :]
        ctx_bank = ps[:, 6, :]
        scale_bank = ps[:, 7, :]
        out_bank = lambda t: ps[:, 7 - t % 2, :]

        def last_user(i):
            return i - BANKS if i >= BANKS else max(k for k in range(-BANKS, 0) if (k + TILES) % BANKS == i)

        block = work.enter_context(nc.Block())

        def over_sequences(eng, step, late):
            step(0, None)
            with eng.Fori(1, B) as b:
                step(b, b - 1)
            for i in range(TILES):
                late(B - 1, i)

        INV_AT = 3
        PV_AT = 6
        SCALE_AT = 8
        CTX_AT = 10
        CUT_AT = 10
        CUT0_AT = 34
        OUT_AT = (16, 19, 26, 30)
        OUT_STEPS = 3
        OUT_TAKE_AT = (18, 21, 29, 33)
        STORE_AT = (12, 12, 14, 15)

        @block.sync
        def _(sp):
            sp.dma_start(staged, chunks(w_o)).then_inc(w_in, 16)
            sp.dma_start(brow[:], row(b_o, H)).then_inc(w_in, 16)
            if not per_seq_mask:
                for t in range(T):
                    sp.dma_start(msk[:, t], mask[0, 0, t * P:(t + 1) * P, :]).then_inc(mask_in[t], 16)

            def late(b, h):
                for t in range(T):
                    if h == STORE_AT[t]:
                        wait(sp, out_ready, b * T + t + 1)
                        sp.dma_start(x_out[b, t * P:(t + 1) * P, :], xo[:, t % 2, :]).then_inc(stored[t % 2], 16)

            def load_mask(b):
                for t in range(T):
                    wait(sp, masked, b * TILES - T + t + 1)
                    sp.dma_start(msk[:, t], mask[b, 0, t * P:(t + 1) * P, :]).then_inc(mask_in[t], 16)

            def step(b, before):
                if per_seq_mask and before is None:
                    load_mask(b)
                for h in range(NH):
                    if per_seq_mask and before is not None and h == SLOTS - 1:
                        load_mask(b)
                    g, j = divmod(h, GH)
                    s, mine = h % SLOTS, slice(j * HD, (j + 1) * HD)
                    wait(sp, scores, b * TILES + (h - SLOTS + 1) * T)
                    q, k = (scratch["heads"][n, b, g, :, mine, :] for n in (q_slot, k_slot))
                    sp.dma_start(qs[0:2 * HD, s].bitcast(F32), q)\
                      .then_inc(head_in[s], 16)
                    sp.dma_start(qs[2 * HD:3 * HD, s].bitcast(F32), q[HI]).then_inc(head_in[s], 16)
                    sp.dma_start(ks[0:HD, s].bitcast(F32), k[HI]).then_inc(head_in[s], 16)
                    sp.dma_start(ks[HD:3 * HD, s].bitcast(F32), k).then_inc(head_in[s], 16)
                    if h == SLOTS - 1:
                        wait(sp, ctx_made, b * G)
                        sp.dma_start(v[:], scratch["v"][b, :, :, :]).then_inc(v_in, 16)
                    if before is not None:
                        late(before, h)
                    if h == NH - 1:
                        wait(sp, out_ready, b * T)
                        sp.dma_start(xt[:], tiles(x, b)).then_inc(x_in, 16)

            over_sequences(sp, step, late)
            for s in stored:
                sp.wait_ge(s, 16 * B * T // 2)

        @block.gpsimd
        def _(pool):
            def spread_group(b, g):
                wait(pool, inv_done, b * G + g + 1)
                wait(pool, scale_turned, b * G + g)
                for t in range(T):
                    pool.tensor_tensor(spread[:, t], inv[:, :, t:t + 1].broadcast_to([P, GH, HD]), ones[:],
                                       ALU.mult).then_inc(spread_done, 1)

            def rest_of_group(b, g):
                wait(pool, ctx_hi, b * G + g + 1)
                pool.tensor_tensor(cT[:, LO, g], cn[:], cT[:, HI, g].bitcast(F32), ALU.subtract).then_inc(ctx_lo, 1)

            def late(b, i):
                if i == 4:
                    spread_group(b, G - 1)
                if i == 8:
                    rest_of_group(b, G - 1)

            def step(b, before):
                if before is not None:
                    late(before, 4)
                    late(before, 8)
                for g in range(G - 1):
                    spread_group(b, g)
                    rest_of_group(b, g)
                wait(pool, x_in, 16 * b + 16)
                for t in range(T):
                    pool.tensor_tensor(xt[:, t, :], xt[:, t, :], brow[:], ALU.add).then_inc(with_bias, 1)

            pool.memset(ones[:], 1.0).then_inc(ones_set, 1)
            pool.wait_ge(ones_set, 1)
            pool.wait_ge(w_in, 32)
            over_sequences(pool, step, late)

        @block.scalar
        def _(act):
            def end_group(b, g, i):
                if i == SCALE_AT:
                    wait(act, scale_turned, b * G + g + 1)
                    wait(act, ctx_done, b * G + g)
                    act.activation(scale[:], scale_bank, ACT.Copy).then_inc(scale_done, 1)
                if i == CUT_AT and g > 0:
                    round_ctx(b, g)

            def round_ctx(b, g):
                wait(act, ctx_done, b * G + g + 1)
                if g == 0:
                    wait(act, out_made, b * T)
                act.activation(cT[:, HI, g], cn[:], ACT.Copy).then_inc(ctx_hi, 1)

            def take(b, n):
                h, t = divmod(n, T)
                g, j = divmod(h, GH)
                if n % (GH * T) == 0:
                    wait(act, ctx_made, b * G + g - 1)
                act.wait_ge(turned, b * TILES + n + 1)
                act.activation(pT[:, g % 2, j, :, t * P:(t + 1) * P],
                               turn_bank(n).rearrange("p (k q) -> p k q", k=T), ACT.Copy).then_inc(taken, 1)

            def late(b, i):
                if i < TAKE_LAG:
                    take(b, TILES - TAKE_LAG + i)
                if i < GH * T:
                    end_group(b, G - 1, i)

            def step(b, before):
                for i in range(TILES):
                    h, t = divmod(i, T)
                    g, j = divmod(h, GH)
                    if t == 0 and j == 0:
                        wait(act, inv_done, b * G + g - 1)
                    act.wait_ge(added, b * TILES + i + 1)
                    act.activation(tile[:, i % RING], tile[:, i % RING], ACT.Exp, scale=-1.0,
                                   bias=least[:, i % RING:i % RING + 1],
                                   accum_out=rowsum[:, g % 2, j, t:t + 1]).then_inc(probs, 1)
                    if before is not None:
                        late(before, i)
                    if i >= TAKE_LAG:
                        take(b, i - TAKE_LAG)
                    if g > 0:
                        end_group(b, g - 1, i % (GH * T))
                    if i == CUT0_AT:
                        round_ctx(b, 0)

            act.wait_ge(w_in, 32)
            act.activation(w[:, HI], staged, ACT.Copy).then_inc(w_hi, 1)
            act.wait_ge(w_lo, 1)
            over_sequences(act, step, late)

        @block.vector
        def _(dve):

            def add(b, n):
                t = n % T
                dve.tensor_tensor_reduce(out=tile[:, n % RING], in0=tile[:, n % RING], in1=away[:, t, :],
                                         scale=1.0, scalar=3.0e38, op0=ALU.add, op1=ALU.min,
                                         accum_out=least[:, n % RING:n % RING + 1]).then_inc(added, 1)

            def end_group(b, g, i):
                if i == INV_AT:
                    wait(dve, probs, b * TILES + (g + 1) * GH * T)
                    wait(dve, spread_done, (b * G + g) * T)
                    dve.reciprocal(inv[:], rowsum[:, g % 2]).then_inc(inv_done, 1)
                if i == CTX_AT:
                    wait(dve, scale_done, b * G + g + 1)
                    wait(dve, ctx_made, b * G + g + 1)
                    wait(dve, ctx_lo, b * G + g)
                    dve.tensor_tensor(cn[:], ctx_bank, scale[:], ALU.mult).then_inc(ctx_done, 1)

            def out_tile(b, t):
                wait(dve, with_bias, b * T + t + 1)
                wait(dve, stored[t % 2], 16 * (b * (T // 2) + t // 2))
                wait(dve, out_made, b * T + t + 1)
                dve.tensor_tensor(xo[:, t % 2], out_bank(t), xt[:, t, :], ALU.add).then_inc(out_ready, 1)

            def late(b, i):
                if i < GH * T:
                    end_group(b, G - 1, i)
                if i in OUT_TAKE_AT:
                    out_tile(b, OUT_TAKE_AT.index(i))

            def last_adds(b):
                hold(dve, masked, b * TILES + TILES, held[:, 0:1])
                for n in range(TILES - ADD_LAG, TILES):
                    add(b, n)

            def make_away(b, t):
                dve.wait_ge(mask_in[t], 16 * b + 16)
                dve.tensor_scalar(away[:, t, :], msk[:, t, :], -10000.0, 10000.0, ALU.mult, ALU.add)\
                   .then_inc(away_done, 1)

            def step(b, before):
                new_mask = per_seq_mask or before is None
                for i in range(TILES):
                    if new_mask and i < T:
                        make_away(b, i)
                    wait(dve, turned, b * TILES + i - RING + 1)
                    wait(dve, scores, b * TILES + i + 1)
                    wait(dve, masked, b * TILES + i - ADD_LAG + 1)
                    if new_mask and ADD_LAG <= i < T + ADD_LAG:
                        dve.wait_ge(away_done, b * T + i - ADD_LAG + 1)
                    dve.scalar_tensor_tensor(tile[:, i % RING], score_bank(i), -float(HD) ** -0.5, msk[:, i % T, :],
                                             ALU.mult, ALU.mult).then_inc(masked, 1)
                    if i >= ADD_LAG:
                        add(b, i - ADD_LAG)
                    elif before is not None:
                        add(before, TILES + i - ADD_LAG)
                    if before is not None:
                        late(before, i)
                    if i >= GH * T:
                        end_group(b, i // (GH * T) - 1, i % (GH * T))

            dve.wait_ge(w_hi, 1)
            dve.tensor_tensor(w[:, LO], staged, w[:, HI].bitcast(F32), ALU.subtract).then_inc(w_lo, 1)
            step(0, None)
            with dve.Fori(1, B) as b:
                step(b, b - 1)
            last_adds(B - 1)
            for i in range(TILES):
                late(B - 1, i)

        @block.tensor
        def _(pe):
            def turn(b, n):
                wait(pe, taken, b * TILES + last_user(n) + 1)
                wait(pe, probs, b * TILES + n + 1)
                for k in range(T):
                    mm = pe.transpose(turn_bank(n)[:, k * P:(k + 1) * P], tile[:, n % RING, k * P:(k + 1) * P], ident[:])
                mm.then_inc(turned, 1)

            def end_group(b, g, i):
                if i == SCALE_AT:
                    wait(pe, spread_done, (b * G + g + 1) * T)
                    if g < 2:
                        wait(pe, out_ready, (b - 1) * T + (1, 3)[g])
                    for t in range(T):
                        mm = pe.transpose(scale_bank[:, t * P:(t + 1) * P],
                                          spread[:, t].rearrange("p j d -> p (j d)"), ident[:])
                    mm.then_inc(scale_turned, 1)
                if PV_AT <= i < PV_AT + T:
                    k = i - PV_AT
                    if k == 0:
                        if g == 0:
                            wait(pe, v_in, 16 * b + 16)
                        wait(pe, ctx_done, b * G + g)
                        if g < 2:
                            wait(pe, out_ready, (b - 1) * T + (2, 4)[g])
                        wait(pe, taken, b * TILES + (g + 1) * GH * T)
                    for j in range(GH):
                        h = g * GH + j
                        mm = pe.matmul(ctx_bank[j * HD:(j + 1) * HD, :], v[:, k, h * HD:(h + 1) * HD],
                                       pT[:, g % 2, j, k, :], start=(k == 0), stop=(k == T - 1))
                    if k == T - 1:
                        mm.then_inc(ctx_made, 1)

            def out_tile(b, t, piece):
                if piece == 0:
                    wait(pe, ctx_lo, b * G + G)
                    next_group = t >= 2 and not isinstance(b, int)
                    wait(pe, (scale_done, ctx_done)[t % 2], b * G + G + next_group)
                    if t >= 2:
                        wait(pe, out_ready, b * T + t - 1)
                passes = [(c, a, m) for c in range(C) for a, m in PASSES]
                count = len(passes) // OUT_STEPS
                for n in range(piece * count, (piece + 1) * count):
                    c, a, m = passes[n]
                    mm = pe.matmul(out_bank(t), cT[:, a, c, t * P:(t + 1) * P], w[:, m, c, :],
                                   start=(n == 0), stop=(n == len(passes) - 1))
                if piece == OUT_STEPS - 1:
                    mm.then_inc(out_made, 1)

            def late(b, i):
                if i < LAG:
                    turn(b, TILES - LAG + i)
                if i < GH * T:
                    end_group(b, G - 1, i)
                for t in range(T):
                    if OUT_AT[t] <= i < OUT_AT[t] + OUT_STEPS:
                        out_tile(b, t, i - OUT_AT[t])

            def step(b, before):
                for i in range(TILES):
                    h, t = divmod(i, T)
                    s = h % SLOTS
                    if t == 0:
                        use = b * (NH // SLOTS) + h // SLOTS + 1
                        pe.wait_ge(head_in[s], 64 * use)
                    wait(pe, masked, b * TILES + last_user(i) + 1)
                    pe.matmul(score_bank(i), qs[:, s, t * P:(t + 1) * P], ks[:, s, :], start=True, stop=True)\
                      .then_inc(scores, 1)
                    if before is not None:
                        late(before, i)
                    if i >= LAG:
                        turn(b, i - LAG)
                    if i >= GH * T:
                        end_group(b, i // (GH * T) - 1, i % (GH * T))

            over_sequences(pe, step, late)

        work.close()
        pl.clear_sems()


def mlp_phase(nc, name, ps, ident, x_in, x, norm, w1, b1, w2, b2, x_out):
    STATS = 2 * T + 1
    PAIRS = M // 2
    with ExitStack() as ctx, ExitStack() as work:
        pl = Place(nc, ctx, name)
        w1s = pl.sb("w1s", [P, 2, C, FF], F32R)
        w2s = pl.sb("w2s", [P, 2, M, H], F32R)
        staged = pl.sb("staged", [P, 2, 2 * H])
        xt = pl.sb("xt", [P, T, H])
        xb = pl.sb("xb", [P, T, H])
        xh = pl.sb("xh", [P, T, H])
        full = pl.sb("full", [P, C, S])
        stats = pl.sb("stats", [P, T, 6])
        mv = pl.sb("mv", [P, T, 2])
        std = pl.sb("std", [P, T])
        rstd = pl.sb("rstd", [P, T])
        eps = pl.sb("eps", [P, 1])
        held = pl.sb("held", [P, 1])
        ln_s = pl.sb("ln_s", [P, C])
        ln_b = pl.sb("ln_b", [P, C])
        b1c = pl.sb("b1c", [P, M])
        brow = pl.sb("brow", [P, H])
        xT = pl.sb("xT", [P, 2, C, S], F32R)
        gel = pl.sb("gel", [P, 2, S])
        hT = pl.sb("hT", [P, 2, 2, S], F32R)
        xo = pl.sb("xo", [P, 2, H])

        par_in = pl.sem("par_in")
        staged_in = [pl.sem(f"staged_in{i}") for i in range(2)]
        w_hi, w_lo = pl.sem("w_hi"), pl.sem("w_lo")
        eps_set, stat, std_done = (pl.sem(n) for n in ("eps_set", "stat", "std_done"))
        normed, turned, full_done, hi_done, cut = (pl.sem(n) for n in ("normed", "turned", "full_done", "hi_done", "cut"))
        chunk_free = pl.sem("chunk_free")
        hid_made = pl.sem("hid_made")
        gel_done = pl.sem("gel_done")
        gel_hi = pl.sem("gel_hi")
        gel_cut = pl.sem("gel_cut")
        hid_used = pl.sem("hid_used")
        tile_made = pl.sem("tile_made")
        with_bias = pl.sem("with_bias")
        out_ready = pl.sem("out_ready")
        stored = [pl.sem(f"stored{i}") for i in range(2)]

        turn_bank = lambda n: ps[:, n % 2, :]
        hid_bank = lambda n: ps[:, 2 + n % 2, :]
        out_bank = lambda t: ps[:, 4 + t, :]
        w1_piece = lambda j, part: w1s[:, part, :, j * 2 * P:(j + 1) * 2 * P]
        w2_piece = lambda j, part: w2s[:, part, 2 * j:2 * j + 2, :].rearrange("p m n -> p (m n)")
        piece = lambda n, part: (w1_piece, w2_piece)[n % 2](n // 2, part)
        staged_piece = lambda n: (staged[:, 0].rearrange("p (c n) -> p c n", c=C), staged[:, 1])[n % 2]
        PREPARE_AT = 2
        TURN_AT = 6
        block = work.enter_context(nc.Block())

        def over_ahead(eng, step):
            step(0, 1)
            with eng.Fori(1, B - 1) as b:
                step(b, b + 1)
            step(B - 1, None)

        @block.sync
        def _(sp):
            for to, src in ((ln_s[:], norm[0]), (ln_b[:], norm[1]), (b1c[:], b1), (brow[:], row(b2, H))):
                sp.dma_start(to, src).then_inc(par_in, 16)
            for n in range(2 * PAIRS):
                wait(sp, w_lo, n - 1)
                j = n // 2
                if n % 2 == 0:
                    sp.dma_start(staged_piece(n), chunks(w1[:, j * 2 * P:(j + 1) * 2 * P])).then_inc(staged_in[0], 16)
                else:
                    sp.dma_start(staged[:, 1].rearrange("p (m n) -> p m n", n=H), chunks(w2[j * 2 * P:(j + 1) * 2 * P, :]))\
                      .then_inc(staged_in[1], 16)

            def step(b):
                for t in range(T):
                    sp.wait_ge(out_ready, b * T + t + 1)
                    sp.dma_start(x_out[b, t * P:(t + 1) * P, :], xo[:, t % 2, :]).then_inc(stored[t % 2], 16)

            over_batch(sp, step)
            for s in stored:
                sp.wait_ge(s, 16 * B * T // 2)

        @block.gpsimd
        def _(pool):
            def add_bias(b):
                wait(pool, out_ready, b * T)
                for t in range(T):
                    pool.tensor_tensor(xb[:, t, :], xt[:, t, :], brow[:], ALU.add).then_inc(with_bias, 1)

            def step(b):
                add_bias(b)
                pool.wait_ge(normed, b * T + T)
                pool.wait_ge(with_bias, b * T + T)
                pool.dma_start(xt[:], tiles(x, b + 1)).then_inc(x_in, 16)
                pool.wait_ge(x_in, 16 * b + 32)

            pool.dma_start(xt[:], tiles(x, 0)).then_inc(x_in, 16)
            pool.wait_ge(par_in, 64)
            pool.wait_ge(x_in, 16)
            step(0)
            with pool.Fori(1, B - 1) as b:
                step(b)
            add_bias(B - 1)

        @block.scalar
        def _(act):
            def root(b):
                act.wait_ge(stat, b * STATS + 2 * T)
                act.activation(std[:], mv[:, :, 1], ACT.Sqrt, bias=eps[:, 0:1]).then_inc(std_done, 1)

            def take(b, c):
                wait(act, cut, (b - 1) * C + c + 1)
                act.wait_ge(turned, b * C + c + 1)
                act.activation(full[:, c], turn_bank(c), ACT.Identity, bias=ln_b[:, c:c + 1],
                               scale=ln_s[:, c:c + 1]).then_inc(full_done, 1)

            def round_chunk(b, c):
                act.wait_ge(full_done, b * C + c + 1)
                if c < C - 1:
                    wait(act, chunk_free, (b - 1) * (C - 1) + c + 1)
                else:
                    wait(act, hid_made, b * M)
                act.activation(xT[:, HI, c], full[:, c], ACT.Copy).then_inc(hi_done, 1)

            def round_weights(n):
                act.wait_ge(staged_in[n % 2], 16 * (n // 2 + 1))
                act.activation(piece(n, HI), staged_piece(n), ACT.Copy).then_inc(w_hi, 1)

            def step(b, ahead):
                for m in range(M):
                    if isinstance(b, int) and b == 0:
                        for n in range(m + 4, m + 5):
                            if n < 2 * PAIRS:
                                round_weights(n)
                    if m == M - 1 and ahead is not None:
                        for c in range(C):
                            round_chunk(ahead, c)
                    n = b * M + m
                    wait(act, gel_cut, n - 1)
                    act.wait_ge(hid_made, n + 1)
                    act.activation(gel[:, m % 2], hid_bank(m), ACT.Gelu_apprx_tanh, bias=b1c[:, m:m + 1])\
                       .then_inc(gel_done, 1)
                    if ahead is not None:
                        if m == PREPARE_AT:
                            root(ahead)
                        if TURN_AT < m <= TURN_AT + C:
                            take(ahead, m - TURN_AT - 1)

            act.wait_ge(par_in, 64)
            act.wait_ge(eps_set, 1)
            root(0)
            for c in range(C):
                take(0, c)
            for c in range(C):
                round_chunk(0, c)
            for n in range(4):
                round_weights(n)
            over_ahead(act, step)

        @block.vector
        def _(dve):
            def statistics(b):
                dve.wait_ge(x_in, 16 * b + 16)
                for t in range(T):
                    dve.bn_stats(stats[:, t, :], xt[:, t, :]).then_inc(stat, 1)
                hold(dve, stat, b * STATS + T, held[:, 0:1])
                for t in range(T):
                    dve.bn_aggr(mv[:, t, :], stats[:, t, :]).then_inc(stat, 1)

            def normalise(b):
                dve.wait_ge(std_done, b + 1)
                dve.reciprocal(rstd[:], std[:]).then_inc(stat, 1)
                dve.wait_ge(stat, b * STATS + STATS)
                wait(dve, turned, b * C)
                for t in range(T):
                    dve.tensor_scalar(xh[:, t, :], xt[:, t, :], mv[:, t, 0:1], rstd[:, t:t + 1],
                                      ALU.subtract, ALU.mult).then_inc(normed, 1)

            def rest_of_chunk(b, c):
                dve.wait_ge(hi_done, b * C + c + 1)
                dve.tensor_tensor(xT[:, LO, c], full[:, c], xT[:, HI, c].bitcast(F32), ALU.subtract)\
                   .then_inc(cut, 1)

            def rest_of_weights(n):
                dve.wait_ge(w_hi, n + 1)
                dve.tensor_tensor(piece(n, LO), staged_piece(n), piece(n, HI).bitcast(F32), ALU.subtract)\
                   .then_inc(w_lo, 1)

            def step(b, ahead):
                for m in range(M):
                    if isinstance(b, int) and b == 0:
                        for n in range(m + 4, m + 5):
                            if n < 2 * PAIRS:
                                rest_of_weights(n)
                    if m == M - 1 and ahead is not None:
                        for c in range(C):
                            rest_of_chunk(ahead, c)
                    n = b * M + m
                    if m >= 2:
                        dve.wait_ge(hid_used, b * (M - 1) + m - 1)
                    dve.wait_ge(gel_done, n + 1)
                    dve.tensor_copy(hT[:, m % 2, HI], gel[:, m % 2]).then_inc(gel_hi, 1)
                    dve.wait_ge(gel_hi, n + 1)
                    dve.tensor_tensor(hT[:, m % 2, LO], gel[:, m % 2], hT[:, m % 2, HI].bitcast(F32), ALU.subtract)\
                       .then_inc(gel_cut, 1)
                    if ahead is not None:
                        if m == PREPARE_AT:
                            statistics(ahead)
                        if m == PREPARE_AT + 1:
                            normalise(ahead)
                dve.wait_ge(with_bias, b * T + T)
                for t in range(T):
                    wait(dve, stored[t % 2], 16 * (b * (T // 2) + t // 2))
                    dve.wait_ge(tile_made, b * T + t + 1)
                    dve.tensor_tensor(xo[:, t % 2], out_bank(t), xb[:, t, :], ALU.add).then_inc(out_ready, 1)

            dve.memset(eps[:], EPS).then_inc(eps_set, 1)
            statistics(0)
            normalise(0)
            for c in range(C):
                rest_of_chunk(0, c)
            for n in range(4):
                rest_of_weights(n)
            over_ahead(dve, step)

        @block.tensor
        def _(pe):
            def turn(b, c):
                if c < 2:
                    wait(pe, full_done, (b - 1) * C + C - 1 + c)
                else:
                    pe.wait_ge(full_done, b * C + c - 1)
                if c == 0:
                    pe.wait_ge(normed, b * T + T)
                for t in range(T):
                    mm = pe.transpose(turn_bank(c)[:, t * P:(t + 1) * P], xh[:, t, c * P:(c + 1) * P], ident[:])
                mm.then_inc(turned, 1)

            def step(b, ahead):
                for m in range(M + 2):
                    if m < M:
                        if isinstance(b, int) and b == 0 and m % 2 == 0:
                            pe.wait_ge(w_lo, m + 1)
                        wait(pe, gel_done, b * M + m - 1)
                        for c in range(C):
                            if m == 0:
                                pe.wait_ge(cut, b * C + c + 1)
                            for n, (a, r) in enumerate(PASSES):
                                mm = pe.matmul(hid_bank(m), w1s[:, a, c, m * P:(m + 1) * P], xT[:, r, c, :],
                                               start=(c == 0 and n == 0), stop=(c == C - 1 and n == 2))
                            if c == C - 1:
                                mm.then_inc(hid_made, 1)
                            elif m == M - 1:
                                mm.then_inc(chunk_free, 1)
                    k = m - 2
                    if k >= 0:
                        if isinstance(b, int) and b == 0 and k % 2 == 0:
                            pe.wait_ge(w_lo, k + 2)
                        pe.wait_ge(gel_cut, b * M + k + 1)
                        for t in range(T):
                            if k == 0:
                                wait(pe, out_ready, (b - 1) * T + t + 1)
                            for n, (a, r) in enumerate(PASSES):
                                mm = pe.matmul(out_bank(t), hT[:, k % 2, a, t * P:(t + 1) * P], w2s[:, r, k, :],
                                               start=(k == 0 and n == 0), stop=(k == M - 1 and n == 2))
                            if k == M - 1:
                                mm.then_inc(tile_made, 1)
                        if k < M - 1:
                            mm.then_inc(hid_used, 1)
                    if ahead is not None and TURN_AT <= m < TURN_AT + C:
                        turn(ahead, m - TURN_AT)

            for c in range(C):
                turn(0, c)
            over_ahead(pe, step)

        work.close()
        pl.clear_sems()


def last_phase(nc, name, ps, ident, x, enc, w_q, w_k, w_v, w_o, alpha, x_out):
    with ExitStack() as ctx, ExitStack() as work:
        pl = Place(nc, ctx, name)
        ws = pl.sb("ws", [P, 4, C, H])
        woT = pl.sb("woT", [P, C, H])
        kq = pl.sb("kq", [P, 2, C, H], F32R)
        vo = pl.sb("vo", [P, 2, C, H], F32R)
        al = pl.sb("al", [P, 1])
        xt = pl.sb("xt", [P, 2, T, H])
        xT = pl.sb("xT", [P, 2, 2, C, S], F32R)
        gT = pl.sb("gT", [P, 2, C, S], F32R)
        u = pl.sb("u", [P, 2, T, H], F32R)
        sc = pl.sb("sc", [P, 4, S])
        least = pl.sb("least", [P, T])
        rowsum = pl.sb("rowsum", [P, T])
        inv = pl.sb("inv", [P, T])
        by = pl.sb("by", [P, T])
        pT = pl.sb("pT", [P, 2, 2, T, P], F32R)
        xo = pl.sb("xo", [P, 2, H])

        w_in = pl.sem("w_in")
        pre_made = pl.sem("pre_made")
        pre_hi = pl.sem("pre_hi")
        pre_done = pl.sem("pre_done")
        x_in, e_in = pl.sem("x_in"), pl.sem("e_in")
        turned = pl.sem("turned")
        turn_hi = pl.sem("turn_hi")
        cut = pl.sem("cut")
        made = pl.sem("made")
        made_hi = pl.sem("made_hi")
        made_cut = pl.sem("made_cut")
        scores = pl.sem("scores")
        least_done = pl.sem("least_done")
        probs = pl.sem("probs")
        inv_done, by_done = pl.sem("inv_done"), pl.sem("by_done")
        p_turned, p_hi, p_cut = pl.sem("p_turned"), pl.sem("p_hi"), pl.sem("p_cut")
        delta = pl.sem("delta")
        out_ready = pl.sem("out_ready")
        stored = [pl.sem(f"stored{i}") for i in range(2)]

        N_PRE = 3 * C
        bank2 = lambda n: ps[:, n % 2, :]
        bank4 = lambda n: ps[:, 4 + n % 4, :]
        score_bank = lambda t: ps[:, 2 + t % 2, :]
        block = work.enter_context(nc.Block())

        @block.sync
        def _(sp):
            for i, w in enumerate((w_q, w_k, w_v, w_o)):
                sp.dma_start(ws[:, i], chunks(w)).then_inc(w_in, 16)
            sp.dma_start(al[:], alpha.rearrange("(a n) -> a n", a=1).broadcast_to([P, 1])).then_inc(w_in, 16)

            def step(b):
                wait(sp, turned, b * 2 * C)
                sp.dma_start(xt[:, 1], tiles(enc, b)).then_inc(e_in, 16)
                wait(sp, out_ready, b * T)
                sp.dma_start(xt[:, 0], tiles(x, b)).then_inc(x_in, 16)
                for t in range(T):
                    sp.wait_ge(out_ready, b * T + t + 1)
                    sp.dma_start(x_out[b, t * P:(t + 1) * P, :], xo[:, t % 2, :]).then_inc(stored[t % 2], 16)

            over_batch(sp, step)
            for s in stored:
                sp.wait_ge(s, 16 * B * T // 2)

        @block.scalar
        def _(act):
            for n in range(N_PRE):
                i, c = divmod(n, C)
                act.wait_ge(pre_made, n + 1)
                to = woT[:, c, :] if i == 0 else (kq, vo)[i - 1][:, HI, c, :]
                act.activation(to, bank4(n), ACT.Copy).then_inc(pre_hi, 1)

            def step(b):
                for n in range(2 * C):
                    act.wait_ge(turned, b * 2 * C + n + 1)
                    if n == 0:
                        wait(act, scores, b * T)
                    act.activation(xT[:, 1 - n // C, HI, n % C], bank2(n), ACT.Copy).then_inc(turn_hi, 1)
                for n in range(2 * C):
                    act.wait_ge(made, b * 2 * C + n + 1)
                    if n == 0:
                        wait(act, delta, b * T)
                    to = gT[:, HI, n, :] if n < C else u[:, HI, n - C, :]
                    act.activation(to, bank4(n), ACT.Copy).then_inc(made_hi, 1)
                for t in range(T):
                    act.wait_ge(least_done, b * T + t + 1)
                    if t == 0:
                        wait(act, inv_done, b)
                    act.activation(sc[:, t], sc[:, t], ACT.Exp, scale=-1.0, bias=least[:, t:t + 1],
                                   accum_out=rowsum[:, t:t + 1]).then_inc(probs, 1)
                for t in range(T):
                    wait(act, delta, b * T + t - 1)
                    act.wait_ge(p_turned, b * T + t + 1)
                    act.activation(pT[:, t % 2, HI].rearrange("p k q -> p (k q)"), bank2(t), ACT.Copy)\
                       .then_inc(p_hi, 1)

            over_batch(act, step)

        @block.vector
        def _(dve):
            dve.wait_ge(w_in, 80)
            for n in range(C, N_PRE):
                i, c = divmod(n, C)
                dve.wait_ge(pre_hi, n + 1)
                w = (kq, vo)[i - 1]
                dve.tensor_tensor(w[:, LO, c, :], bank4(n), w[:, HI, c, :].bitcast(F32), ALU.subtract)\
                   .then_inc(pre_done, 1)

            def step(b):
                for n in range(2 * C):
                    which = 1 - n // C
                    dve.wait_ge(turn_hi, b * 2 * C + n + 1)
                    dve.tensor_tensor(xT[:, which, LO, n % C], bank2(n), xT[:, which, HI, n % C].bitcast(F32),
                                      ALU.subtract).then_inc(cut, 1)
                for n in range(2 * C):
                    dve.wait_ge(made_hi, b * 2 * C + n + 1)
                    to = gT[:, :, n, :] if n < C else u[:, :, n - C, :]
                    dve.tensor_tensor(to[:, LO], bank4(n), to[:, HI].bitcast(F32), ALU.subtract).then_inc(made_cut, 1)
                for t in range(T):
                    dve.wait_ge(scores, b * T + t + 1)
                    wait(dve, p_turned, b * T)
                    dve.tensor_scalar(sc[:, t], score_bank(t), -float(H) ** -0.5, None, ALU.mult, ALU.min,
                                      accum_out=least[:, t:t + 1]).then_inc(least_done, 1)
                dve.wait_ge(probs, b * T + T)
                dve.reciprocal(inv[:], rowsum[:]).then_inc(inv_done, 1)
                dve.wait_ge(inv_done, b + 1)
                dve.tensor_scalar(by[:], inv[:], al[:, 0:1], None, ALU.mult).then_inc(by_done, 1)
                for t in range(T + 1):
                    if t < T:
                        dve.wait_ge(p_hi, b * T + t + 1)
                        dve.tensor_tensor(pT[:, t % 2, LO].rearrange("p k q -> p (k q)"), bank2(t),
                                          pT[:, t % 2, HI].rearrange("p k q -> p (k q)").bitcast(F32),
                                          ALU.subtract).then_inc(p_cut, 1)
                    if t == 0:
                        dve.wait_ge(by_done, b + 1)
                    else:
                        k = t - 1
                        wait(dve, stored[k % 2], 16 * (b * (T // 2) + k // 2))
                        dve.wait_ge(delta, b * T + k + 1)
                        dve.scalar_tensor_tensor(xo[:, k % 2], bank4(k), by[:, k:k + 1], xt[:, 0, k, :],
                                                 ALU.mult, ALU.add).then_inc(out_ready, 1)

            over_batch(dve, step)

        @block.tensor
        def _(pe):
            pe.wait_ge(w_in, 80)
            for n in range(N_PRE):
                i, c = divmod(n, C)
                if C <= n - 4:
                    pe.wait_ge(pre_done, n - 4 - C + 1)
                elif n >= 4:
                    pe.wait_ge(pre_hi, n - 3)
                if i == 0:
                    for k in range(C):
                        mm = pe.transpose(bank4(n)[:, k * P:(k + 1) * P], ws[:, 3, k, c * P:(c + 1) * P], ident[:])
                else:
                    if i == 2 and c == 0:
                        pe.wait_ge(pre_hi, C)
                    for k in range(C):
                        if i == 1:
                            lhsT, rhs = ws[:, 1, k, c * P:(c + 1) * P], ws[:, 0, k, :]
                        else:
                            lhsT, rhs = ws[:, 2, k, c * P:(c + 1) * P], woT[:, k, :]
                        mm = pe.matmul(bank4(n), lhsT, rhs, start=(k == 0), stop=(k == C - 1))
                mm.then_inc(pre_made, 1)
            pe.wait_ge(pre_done, 2 * C)

            def product(bank, stationary, moving):
                n = 0
                for c in range(C):
                    for a, r in PASSES:
                        mm = pe.matmul(bank, stationary(a, c), moving(r, c), start=(n == 0), stop=(n == 3 * C - 1))
                        n += 1
                return mm

            def step(b):
                for n in range(2 * C):
                    which, c = 1 - n // C, n % C
                    if n == 0:
                        pe.wait_ge(e_in, 16 * b + 16)
                        wait(pe, p_cut, b * T)
                    if n == C:
                        pe.wait_ge(x_in, 16 * b + 16)
                    wait(pe, cut, b * 2 * C + n - 1)
                    for t in range(T):
                        mm = pe.transpose(bank2(n)[:, t * P:(t + 1) * P], xt[:, which, t, c * P:(c + 1) * P], ident[:])
                    mm.then_inc(turned, 1)
                pe.wait_ge(cut, b * 2 * C + 2 * C)
                for n in range(2 * C):
                    wait(pe, made_cut, b * 2 * C + n - 3)
                    wait(pe, out_ready, b * T)
                    part = slice((n % C) * P, (n % C + 1) * P)
                    if n < C:
                        mm = product(bank4(n), lambda a, c: kq[:, a, c, part], lambda r, c: xT[:, 1, r, c, :])
                    else:
                        mm = product(bank4(n), lambda a, c: xT[:, 1, a, c, part], lambda r, c: vo[:, r, c, :])
                    mm.then_inc(made, 1)
                for t in range(T):
                    pe.wait_ge(made_cut, b * 2 * C + C)
                    wait(pe, least_done, b * T + t - 1)
                    part = slice(t * P, (t + 1) * P)
                    product(score_bank(t), lambda a, c: xT[:, 0, a, c, part], lambda r, c: gT[:, r, c, :])\
                        .then_inc(scores, 1)
                pe.wait_ge(made_cut, b * 2 * C + 2 * C)

                def turn(t):
                    pe.wait_ge(probs, b * T + t + 1)
                    wait(pe, p_cut, b * T + t - 1)
                    for k in range(T):
                        mm = pe.transpose(bank2(t)[:, k * P:(k + 1) * P], sc[:, t, k * P:(k + 1) * P], ident[:])
                    mm.then_inc(p_turned, 1)

                turn(0)
                for t in range(T):
                    if t + 1 < T:
                        turn(t + 1)
                    pe.wait_ge(p_cut, b * T + t + 1)
                    product(bank4(t), lambda a, c: pT[:, t % 2, a, c, :], lambda r, c: u[:, r, c, :]).then_inc(delta, 1)

            over_batch(pe, step)


def layer_and_cross_attention_kernel(nc, a, out):
    with ExitStack() as ctx:
        scratch = {
            "heads": nc.dram_tensor("heads", [4, B, G, 2, P, S], F32, kind="Internal").ap(),
            "v": nc.dram_tensor("v_scratch", [B, P, T, H], F32, kind="Internal").ap(),
        }
        cross = {
            "heads": scratch["heads"],
            "v": nc.dram_tensor("cross_v_scratch", [B, P, T, H], F32, kind="Internal").ap(),
        }
        x1 = nc.dram_tensor("x1", [B, S, H], F32, kind="Internal").ap()
        x2 = nc.dram_tensor("x2", [B, S, H], F32, kind="Internal").ap()
        x3 = nc.dram_tensor("x3", [B, S, H], F32, kind="Internal").ap()
        ps = ctx.enter_context(nc.psum_tensor("ps", [P, 8, S], F32))
        ident = ctx.enter_context(nc.sbuf_tensor("ident", [P, P], F32))
        zeroed = ctx.enter_context(nc.semaphore("zeroed"))
        ident_set = ctx.enter_context(nc.semaphore("ident_set"))

        x_in = {n: ctx.enter_context(nc.semaphore(f"{n}_x_in")) for n in ("self_qkv", "cross_kv", "cross_q", "mlp")}

        with nc.Block() as block:
            @block.gpsimd
            def _(pool):
                nc.gpsimd.memset(ident[:], 0.0).then_inc(zeroed, 1)
                pool.wait_ge(zeroed, 1)
                nc.gpsimd.affine_select(out=ident[:], in_=ident[:], compare_op=ALU.not_equal, fill=1.0, base=0,
                                        pattern=[[-1, P]], channel_multiplier=1).then_inc(ident_set, 1)
                pool.wait_ge(ident_set, 1)

        cqkv, ckv = a["columns_L0_xattn_b_qkv"], a["columns_L0_xattn_b_kv"]
        col = lambda v, i: v[:, i * C:(i + 1) * C]
        wqkv, wkv = a["L0_xattn_w_qkv"], a["L0_xattn_w_kv"]
        bqkv, bkv = a["L0_xattn_b_qkv"], a["L0_xattn_b_kv"]
        cut = lambda w, i: w[:, i * H:(i + 1) * H]
        vec = lambda v, i: v[i * H:(i + 1) * H]
        project_phase(nc, "self_qkv", ps, ident, x_in["self_qkv"], a["x"], (a["columns_L0_xattn_ln1_s"], a["columns_L0_xattn_ln1_b"]),
                      [(cut(wqkv, 0), col(cqkv, 0), 0), (cut(wqkv, 1), col(cqkv, 1), 1)],
                      [(cut(wqkv, 2), vec(bqkv, 2))], scratch)
        project_phase(nc, "cross_kv", ps, ident, x_in["cross_kv"], a["ctx_2048"], None,
                      [(cut(wkv, 0), col(ckv, 0), 3)], [(cut(wkv, 1), vec(bkv, 1))], cross)
        attention_phase(nc, "self_att", ps, ident, scratch, 0, 1, a["mask_1x1xSxS2_fc1"], a["L0_xattn_w_ao"],
                        a["L0_xattn_b_ao"], a["x"], x1)
        project_phase(nc, "cross_q", ps, ident, x_in["cross_q"], x1, (a["columns_L0_xattn_ln2_s"], a["columns_L0_xattn_ln2_b"]),
                      [(a["L0_xattn_w_q"], a["columns_L0_xattn_b_q"], 2)], [], cross)
        attention_phase(nc, "cross_att", ps, ident, cross, 2, 3, a["mask_Bx1xSxS2_ff1"], a["L0_xattn_w_co"],
                        a["L0_xattn_b_co"], x1, x2)
        mlp_phase(nc, "mlp", ps, ident, x_in["mlp"], x2, (a["columns_L0_xattn_ln3_s"], a["columns_L0_xattn_ln3_b"]), a["L0_xattn_w1"],
                  a["columns_L0_xattn_b1"], a["L0_xattn_w2"], a["L0_xattn_b2"], x3)
        last_phase(nc, "last", ps, ident, x3, a["ctx_2048"], a["L1_xattn_w_q"], a["L1_xattn_w_k"],
                   a["L1_xattn_w_v"], a["L1_xattn_w_o"], a["L1_xattn_alpha"], out)


_INS = ["x", "ctx_2048", "mask_1x1xSxS2_fc1", "mask_Bx1xSxS2_ff1", "L0_xattn_ln1_s", "L0_xattn_ln1_b",
        "L0_xattn_w_qkv", "L0_xattn_b_qkv", "L0_xattn_w_ao", "L0_xattn_b_ao", "L0_xattn_ln2_s", "L0_xattn_ln2_b",
        "L0_xattn_w_q", "L0_xattn_b_q", "L0_xattn_w_kv", "L0_xattn_b_kv", "L0_xattn_w_co", "L0_xattn_b_co",
        "L0_xattn_ln3_s", "L0_xattn_ln3_b", "L0_xattn_w1", "L0_xattn_b1", "L0_xattn_w2", "L0_xattn_b2",
        "L1_xattn_w_q", "L1_xattn_w_k", "L1_xattn_w_v", "L1_xattn_w_o", "L1_xattn_alpha"]

_COLUMNS = ["L0_xattn_ln1_s", "L0_xattn_ln1_b", "L0_xattn_b_qkv", "L0_xattn_ln2_s", "L0_xattn_ln2_b",
            "L0_xattn_b_q", "L0_xattn_b_kv", "L0_xattn_ln3_s", "L0_xattn_ln3_b", "L0_xattn_b1"]


def kernel(**inputs):
    import numpy as _np
    import concourse.bacc as _bacc
    from concourse import mybir as _mybir
    from concourse.bass_utils import run_bass_kernel_spmd as _run

    nc = _bacc.Bacc("TRN2", target_bir_lowering=False, num_devices=1)
    arrays, args = {}, {}
    given = {name: _np.asarray(inputs[name]).reshape(inputs[name].shape or (1,)) for name in _INS}
    given |= {f"columns_{name}": given[name].reshape(-1, P).T for name in _COLUMNS}
    for name, a in given.items():
        a = _np.ascontiguousarray(a)
        arrays[f"in_{name}"] = a
        args[name] = nc.dram_tensor(f"in_{name}", a.shape, _mybir.dt.from_np(a.dtype), kind="ExternalInput").ap()
    out = nc.dram_tensor("out_0", (B, S, H), F32, kind="ExternalOutput").ap()
    layer_and_cross_attention_kernel(nc, args, out)
    r = _run(nc, [arrays], core_ids=[0])
    return r.results[0]["out_0"]
```

```python
from contextlib import ExitStack

import concourse.bass as bass
from concourse import mybir

F32 = mybir.dt.float32
F32R = mybir.dt.float32r
ALU = mybir.AluOpType
ACT = mybir.ActivationFunctionType

P = 128
B, S, H = 4, 512, 512
NH, HD = 16, 32
T = S // P
C = H // P
FF = 4 * H
M = FF // P
GH = P // HD
G = NH // GH
TILES = NH * T
EPS = 1e-5
HI, LO = 0, 1
K, Q = 0, 1
PASSES = ((HI, HI), (LO, HI), (HI, LO))


def wait(eng, sem, value):
    if not isinstance(value, int) or value > 0:
        eng.wait_ge(sem, value)


def hold(dve, sem, value, cell):
    wait(dve, sem, value)
    dve.memset(cell, 0.0)


def over_batch(eng, step):
    step(0)
    with eng.Fori(1, B) as b:
        step(b)


class Place:

    def __init__(self, nc, ctx, phase):
        self.nc, self.ctx, self.phase, self.sems = nc, ctx, phase, []

    def sb(self, name, shape, dt=F32):
        return self.ctx.enter_context(self.nc.sbuf_tensor(f"{self.phase}_{name}", shape, dt))

    def sem(self, name):
        self.sems.append(self.ctx.enter_context(self.nc.semaphore(f"{self.phase}_{name}")))
        return self.sems[-1]

    def clear_sems(self):
        with self.nc.Block() as block:
            @block.sync
            def _(sp):
                for s in self.sems:
                    sp.sem_clear(s)


def chunks(w):
    return w.rearrange("(c p) n -> p c n", p=P)


def tiles(x, b):
    return x[b, :, :].rearrange("(t p) n -> p t n", p=P)


def row(v, n):
    return v.rearrange("(a n) -> a n", a=1).broadcast_to([P, n])


def project_phase(nc, name, ps, ident, x_in, sources, scratch):
    ns = len(sources)
    blocks = [block for _, _, own in sources for block in own]
    nb = len(blocks)
    outs = nb * G
    first = [G * sum(len(own) for _, _, own in sources[:s]) for s in range(ns + 1)]
    to_round = [n for n in range(outs) if blocks[n // G][2] is not None]
    STATS = 2 * T + 1
    with ExitStack() as ctx, ExitStack() as work:
        pl = Place(nc, ctx, name)
        staged = pl.sb("staged", [P, nb, C, H])
        w = pl.sb("w", [P, nb, 2, C, H], F32R)
        xt = [pl.sb(f"xt{s}", [P, T, H]) for s in range(ns)]
        xh = [pl.sb(f"xh{s}", [P, T, H]) if sources[s][1] else xt[s] for s in range(ns)]
        stats = pl.sb("stats", [P, T, 6])
        mv = pl.sb("mv", [P, T, 2])
        std = pl.sb("std", [P, T])
        rstd = pl.sb("rstd", [P, T])
        eps = pl.sb("eps", [P, 1])
        held = pl.sb("held", [P, 1])
        ln_s = pl.sb("ln_s", [P, C])
        ln_b = pl.sb("ln_b", [P, C])
        full = [pl.sb(f"full{s}", [P, C, S]) for s in range(ns)]
        xT = [pl.sb(f"xT{s}", [P, 2, C, S], F32R) for s in range(ns)]
        bcol = pl.sb("bcol", [P, nb, G])
        brow = pl.sb("brow", [P, H])
        out = pl.sb("out", [P, 4, 2, S], F32R)

        each = lambda what: [pl.sem(f"{what}{s}") for s in range(ns)]
        ln_in = pl.sem("ln_in")
        bias_in = pl.sem("bias_in")
        w_in = [pl.sem(f"w_in{i}") for i in range(nb)]
        w_hi = pl.sem("w_hi")
        w_lo = pl.sem("w_lo")
        x_in = [x_in] + [pl.sem(f"x_in{s}") for s in range(1, ns)]
        eps_set = pl.sem("eps_set")
        stat = pl.sem("stat")
        std_done = pl.sem("std_done")
        normed = pl.sem("normed")
        turned = each("turned")
        full_done = each("full_done")
        hi_done = each("hi_done")
        cut = each("cut")
        chunk_free = each("chunk_free")
        made = pl.sem("made")
        rounded = pl.sem("rounded")
        ready = pl.sem("ready")
        stored = [pl.sem(f"stored{i}") for i in range(4)]

        turn_bank = lambda n: ps[:, n % 4, :]
        made_bank = lambda n: ps[:, 4 + n % 4, :]
        block = work.enter_context(nc.Block())

        def source_of(n):
            return max(s for s in range(ns) if first[s] <= n)

        def following(s, b, ahead):
            if s + 1 < ns:
                return s + 1, b
            return None if ahead is None else (0, ahead)

        def turn_at(s):
            count = first[s + 1] - first[s]
            start = count // 2 if sources[(s + 1) % ns][1] else 0
            return [first[s] + start + c // 2 for c in range(C)]

        def over_ahead(eng, step):
            step(0, 1)
            with eng.Fori(1, B - 1) as b:
                step(b, b + 1)
            step(B - 1, None)

        @block.sync
        def _(sp):
            for _, norm, _ in sources:
                if norm:
                    sp.dma_start(ln_s[:], norm[0]).then_inc(ln_in, 16)
                    sp.dma_start(ln_b[:], norm[1]).then_inc(ln_in, 16)
            for i, (weights, bias, slot) in enumerate(blocks):
                sp.dma_start(staged[:, i], chunks(weights)).then_inc(w_in[i], 16)
                if slot is not None:
                    sp.dma_start(bcol[:, i, :], bias).then_inc(bias_in, 16)
                else:
                    sp.dma_start(brow[:], row(bias, H)).then_inc(bias_in, 16)

            for s in range(1, ns):
                sp.dma_start(xt[s][:], tiles(sources[s][0], 0)).then_inc(x_in[s], 16)

            def step(b, ahead):
                for n in range(outs):
                    if ahead is not None:
                        for s in range(1, ns):
                            if n == first[s]:
                                if sources[s][1]:
                                    sp.wait_ge(normed, b * T + T)
                                else:
                                    sp.wait_ge(turned[s], b * C + C)
                                sp.dma_start(xt[s][:], tiles(sources[s][0], ahead)).then_inc(x_in[s], 16)
                    wait(sp, ready, b * outs + n + 1)
                    blk, g = divmod(n, G)
                    slot = blocks[blk][2]
                    if slot is not None:
                        to = scratch["heads"][slot, b, g, :, :, :]
                        sp.dma_start(to.rearrange("k p n -> p k n"), out[:, n % 4].bitcast(F32))\
                          .then_inc(stored[n % 4], 16)
                    else:
                        sp.dma_start(scratch["v"][b, :, g, :], out[:, n % 4, 0, :].bitcast(F32))\
                          .then_inc(stored[n % 4], 16)

            over_ahead(sp, step)
            for s in stored:
                sp.wait_ge(s, 16 * B * outs // 4)

        @block.gpsimd
        def _(pool):
            pool.dma_start(xt[0][:], tiles(sources[0][0], 0)).then_inc(x_in[0], 16)
            with pool.Fori(1, B) as b:
                if sources[0][1]:
                    pool.wait_ge(normed, b * T)
                else:
                    pool.wait_ge(turned[0], b * C)
                pool.dma_start(xt[0][:], tiles(sources[0][0], b)).then_inc(x_in[0], 16)

        @block.scalar
        def _(act):
            def root(b):
                act.wait_ge(stat, b * STATS + 2 * T)
                act.activation(std[:], mv[:, :, 1], ACT.Sqrt, bias=eps[:, 0:1]).then_inc(std_done, 1)

            def take(s, b, c):
                wait(act, cut[s], (b - 1) * C + c + 1)
                act.wait_ge(turned[s], b * C + c + 1)
                if sources[s][1]:
                    act.activation(full[s][:, c], turn_bank(c), ACT.Identity, bias=ln_b[:, c:c + 1],
                                   scale=ln_s[:, c:c + 1]).then_inc(full_done[s], 1)
                else:
                    act.activation(full[s][:, c], turn_bank(c), ACT.Copy).then_inc(full_done[s], 1)

            def round_chunk(s, b, c):
                act.wait_ge(full_done[s], b * C + c + 1)
                if c < C - 1:
                    wait(act, chunk_free[s], (b - 1) * (C - 1) + c + 1)
                else:
                    wait(act, made, (b - 1) * outs + first[s + 1])
                act.activation(xT[s][:, HI, c], full[s][:, c], ACT.Copy).then_inc(hi_done[s], 1)

            def step(b, ahead):
                for n in range(outs):
                    s = source_of(n)
                    to_do = following(s, b, ahead)
                    if n == first[s + 1] - 1 and to_do:
                        for c in range(C):
                            if turn_at(s)[c] >= n - 1:
                                take(*to_do, c)
                        for c in range(C):
                            round_chunk(*to_do, c)
                    if n in to_round:
                        blk, g = divmod(n, G)
                        wait(act, stored[n % 4], 16 * (b * (outs // 4) + n // 4))
                        act.wait_ge(made, b * outs + n + 1)
                        act.activation(out[:, n % 4, HI], made_bank(n), ACT.Identity, bias=bcol[:, blk, g:g + 1])\
                           .then_inc(rounded, 1)
                    if to_do:
                        if n == first[s] and sources[to_do[0]][1]:
                            root(to_do[1])
                        if n < first[s + 1] - 1:
                            for c in range(C):
                                if turn_at(s)[c] + 1 == n:
                                    take(*to_do, c)

            def round_weights(i):
                act.wait_ge(w_in[i], 16)
                act.activation(w[:, i, HI], staged[:, i], ACT.Copy).then_inc(w_hi, 1)

            act.wait_ge(eps_set, 1)
            if sources[0][1]:
                act.wait_ge(ln_in, 32)
                root(0)
            round_weights(0)
            for c in range(C):
                take(0, 0, c)
            for c in range(C):
                round_chunk(0, 0, c)
            for i in range(1, nb):
                round_weights(i)
            act.wait_ge(bias_in, 16 * nb)
            act.wait_ge(ln_in, 32)
            over_ahead(act, step)

        @block.vector
        def _(dve):
            def statistics(s, b):
                dve.wait_ge(x_in[s], 16 * b + 16)
                for t in range(T):
                    dve.bn_stats(stats[:, t, :], xt[s][:, t, :]).then_inc(stat, 1)
                hold(dve, stat, b * STATS + T, held[:, 0:1])
                for t in range(T):
                    dve.bn_aggr(mv[:, t, :], stats[:, t, :]).then_inc(stat, 1)

            def normalise(s, b):
                dve.wait_ge(std_done, b + 1)
                dve.reciprocal(rstd[:], std[:]).then_inc(stat, 1)
                dve.wait_ge(stat, b * STATS + STATS)
                wait(dve, turned[s], b * C)
                for t in range(T):
                    dve.tensor_scalar(xh[s][:, t, :], xt[s][:, t, :], mv[:, t, 0:1], rstd[:, t:t + 1],
                                      ALU.subtract, ALU.mult).then_inc(normed, 1)

            def rest_of_chunk(s, b, c):
                dve.wait_ge(hi_done[s], b * C + c + 1)
                dve.tensor_tensor(xT[s][:, LO, c], full[s][:, c], xT[s][:, HI, c].bitcast(F32), ALU.subtract)\
                   .then_inc(cut[s], 1)

            def step(b, ahead):
                for n in range(outs):
                    s = source_of(n)
                    to_do = following(s, b, ahead)
                    if n == first[s + 1] - 1 and to_do:
                        for c in range(C):
                            rest_of_chunk(*to_do, c)
                    if n in to_round:
                        blk, g = divmod(n, G)
                        dve.wait_ge(rounded, b * len(to_round) + to_round.index(n) + 1)
                        dve.scalar_tensor_tensor(out[:, n % 4, LO], made_bank(n), bcol[:, blk, g:g + 1],
                                                 out[:, n % 4, HI].bitcast(F32), ALU.add, ALU.subtract)\
                           .then_inc(ready, 1)
                    else:
                        wait(dve, stored[n % 4], 16 * (b * (outs // 4) + n // 4))
                        dve.wait_ge(made, b * outs + n + 1)
                        dve.tensor_tensor(out[:, n % 4, 0].bitcast(F32), made_bank(n), brow[:], ALU.add)\
                           .then_inc(ready, 1)
                    if to_do and sources[to_do[0]][1]:
                        if n == first[s]:
                            statistics(*to_do)
                        if n == first[s] + 1:
                            normalise(*to_do)

            def rest_of_weights(i):
                dve.wait_ge(w_hi, i + 1)
                dve.tensor_tensor(w[:, i, LO], staged[:, i], w[:, i, HI].bitcast(F32), ALU.subtract)\
                   .then_inc(w_lo, 1)

            dve.memset(eps[:], EPS).then_inc(eps_set, 1)
            if sources[0][1]:
                statistics(0, 0)
                normalise(0, 0)
            rest_of_weights(0)
            for c in range(C):
                rest_of_chunk(0, 0, c)
            for i in range(1, nb):
                rest_of_weights(i)
            dve.wait_ge(bias_in, 16 * nb)
            over_ahead(dve, step)

        @block.tensor
        def _(pe):
            def turn(s, b, c):
                if s > 0:
                    pe.wait_ge(full_done[s - 1], b * C + c + 1)
                else:
                    wait(pe, full_done[ns - 1], (b - 1) * C + c + 1)
                if c == 0:
                    if sources[s][1]:
                        pe.wait_ge(normed, b * T + T)
                    else:
                        pe.wait_ge(x_in[s], 16 * b + 16)
                for t in range(T):
                    mm = pe.transpose(turn_bank(c)[:, t * P:(t + 1) * P], xh[s][:, t, c * P:(c + 1) * P], ident[:])
                mm.then_inc(turned[s], 1)

            def step(b, ahead):
                for n in range(outs):
                    s = source_of(n)
                    to_do = following(s, b, ahead)
                    blk, g = divmod(n, G)
                    part = slice(g * P, (g + 1) * P)
                    if isinstance(b, int) and b == 0 and g == 0:
                        pe.wait_ge(w_lo, blk + 1)
                    wait(pe, ready, b * outs + n - 3)
                    for c in range(C):
                        if n == first[s]:
                            pe.wait_ge(cut[s], b * C + c + 1)
                        for k, (a, m) in enumerate(PASSES):
                            if blocks[blk][2] is not None:
                                lhsT, rhs = w[:, blk, a, c, part], xT[s][:, m, c, :]
                            else:
                                lhsT, rhs = xT[s][:, a, c, part], w[:, blk, m, c, :]
                            mm = pe.matmul(made_bank(n), lhsT, rhs, start=(c == 0 and k == 0),
                                           stop=(c == C - 1 and k == 2))
                        if c == C - 1:
                            mm.then_inc(made, 1)
                        elif n == first[s + 1] - 1:
                            mm.then_inc(chunk_free[s], 1)
                    for c in range(C):
                        if to_do and turn_at(s)[c] == n:
                            turn(*to_do, c)

            for c in range(C):
                turn(0, 0, c)
            over_ahead(pe, step)

        work.close()
        pl.clear_sems()


def attention_phase(nc, name, ps, ident, scratch, q_slot, k_slot, mask, w_o, b_o, x, x_out):
    per_seq_mask = mask.shape[0] == B
    SLOTS = 8
    RING = 8
    BANKS = 2
    TURN_BANKS = 4
    ADD_LAG = 1
    LAG = 5
    TAKE_LAG = LAG - 2
    with ExitStack() as ctx, ExitStack() as work:
        pl = Place(nc, ctx, name)
        qs = pl.sb("qs", [3 * HD, SLOTS, S], F32R)
        ks = pl.sb("ks", [3 * HD, SLOTS, S], F32R)
        v = pl.sb("v", [P, T, H])
        msk = pl.sb("msk", [P, T, S])
        away = pl.sb("away", [P, T, S])
        tile = pl.sb("tile", [P, RING, S])
        least = pl.sb("least", [P, RING])
        held = pl.sb("held", [P, 2])
        rowsum = pl.sb("rowsum", [P, 2, GH, T])
        inv = pl.sb("inv", [P, GH, T])
        spread = pl.sb("spread", [P, T, GH, HD])
        ones = pl.sb("ones", [P, GH, HD])
        scale = pl.sb("scale", [P, S])
        pT = pl.sb("pT", [P, 2, GH, T, S])
        cn = pl.sb("cn", [P, S])
        cT = pl.sb("cT", [P, 2, G, S], F32R)
        w = pl.sb("w", [P, 2, C, H], F32R)
        xt = pl.sb("xt", [P, T, H])
        brow = pl.sb("brow", [P, H])
        xo = pl.sb("xo", [P, 2, H])
        staged = pT[:, 0, :, 0, :]

        w_in, w_hi, w_lo = pl.sem("w_in"), pl.sem("w_hi"), pl.sem("w_lo")
        head_in = [pl.sem(f"head_in{i}") for i in range(SLOTS)]
        v_in, x_in = pl.sem("v_in"), pl.sem("x_in")
        mask_in = [pl.sem(f"mask_in{t}") for t in range(T)]
        away_done = pl.sem("away_done")
        scores = pl.sem("scores")
        masked = pl.sem("masked")
        added = pl.sem("added")
        probs = pl.sem("probs")
        turned = pl.sem("turned")
        taken = pl.sem("taken")
        ones_set = pl.sem("ones_set")
        inv_done = pl.sem("inv_done")
        spread_done = pl.sem("spread_done")
        scale_turned = pl.sem("scale_turned")
        scale_done = pl.sem("scale_done")
        ctx_made = pl.sem("ctx_made")
        ctx_done = pl.sem("ctx_done")
        ctx_hi, ctx_lo = pl.sem("ctx_hi"), pl.sem("ctx_lo")
        with_bias = pl.sem("with_bias")
        out_made = pl.sem("out_made")
        out_ready = pl.sem("out_ready")
        stored = [pl.sem(f"stored{i}") for i in range(2)]

        score_bank = lambda i: ps[:, i % BANKS, :]
        turn_bank = lambda i: ps[:, BANKS + i % TURN_BANKS, :]
        ctx_bank = ps[:, 6, :]
        scale_bank = ps[:, 7, :]
        out_bank = lambda t: ps[:, 7 - t % 2, :]
        last_bank = lambda t: ps[:, t, :]

        block = work.enter_context(nc.Block())

        def over_sequences(eng, step, late):
            step(0, None)
            with eng.Fori(1, B) as b:
                step(b, b - 1)
            for i in range(TILES):
                late(B - 1, i)

        INV_AT = 2
        PV_AT = 7
        SCALE_AT = 8
        CTX_AT = 10
        CUT_AT = 10
        CUT0_AT = 34
        OUT_AT = (15, 18, 27, 31)
        OUT_STEPS = 3
        OUT_TAKE_AT = (17, 20, 29, 33)
        OUT_PASSES = [(c, a, m) for c in range(C) for a, m in PASSES]
        STORE_AT = (12, 12, 14, 15)

        @block.sync
        def _(sp):
            sp.dma_start(staged, chunks(w_o)).then_inc(w_in, 16)
            sp.dma_start(brow[:], row(b_o, H)).then_inc(w_in, 16)
            if not per_seq_mask:
                for t in range(T):
                    sp.dma_start(msk[:, t], mask[0, 0, t * P:(t + 1) * P, :]).then_inc(mask_in[t], 16)

            def late(b, h):
                for t in range(T):
                    if h == STORE_AT[t]:
                        wait(sp, out_ready, b * T + t + 1)
                        sp.dma_start(x_out[b, t * P:(t + 1) * P, :], xo[:, t % 2, :]).then_inc(stored[t % 2], 16)

            def load_mask(b):
                for t in range(T):
                    wait(sp, masked, b * TILES - T + t + 1)
                    sp.dma_start(msk[:, t], mask[b, 0, t * P:(t + 1) * P, :]).then_inc(mask_in[t], 16)

            def step(b, before):
                if per_seq_mask and before is None:
                    load_mask(b)
                for h in range(NH):
                    if per_seq_mask and before is not None and h == SLOTS - 1:
                        load_mask(b)
                    g, j = divmod(h, GH)
                    s, mine = h % SLOTS, slice(j * HD, (j + 1) * HD)
                    wait(sp, scores, b * TILES + (h - SLOTS + 1) * T)
                    q, k = (scratch["heads"][n, b, g, :, mine, :] for n in (q_slot, k_slot))
                    sp.dma_start(qs[0:2 * HD, s].bitcast(F32), q)\
                      .then_inc(head_in[s], 16)
                    sp.dma_start(qs[2 * HD:3 * HD, s].bitcast(F32), q[HI]).then_inc(head_in[s], 16)
                    sp.dma_start(ks[0:HD, s].bitcast(F32), k[HI]).then_inc(head_in[s], 16)
                    sp.dma_start(ks[HD:3 * HD, s].bitcast(F32), k).then_inc(head_in[s], 16)
                    if h == SLOTS - 1:
                        wait(sp, ctx_made, b * G)
                        sp.dma_start(v[:], scratch["v"][b, :, :, :]).then_inc(v_in, 16)
                    if before is not None:
                        late(before, h)
                    if h == NH - 1:
                        wait(sp, out_ready, b * T)
                        sp.dma_start(xt[:], tiles(x, b)).then_inc(x_in, 16)

            over_sequences(sp, step, late)
            for s in stored:
                sp.wait_ge(s, 16 * B * T // 2)

        @block.gpsimd
        def _(pool):
            def spread_group(b, g):
                wait(pool, inv_done, b * G + g + 1)
                wait(pool, scale_turned, b * G + g)
                for t in range(T):
                    pool.tensor_tensor(spread[:, t], inv[:, :, t:t + 1].broadcast_to([P, GH, HD]), ones[:],
                                       ALU.mult).then_inc(spread_done, 1)

            def rest_of_group(b, g):
                wait(pool, ctx_hi, b * G + g + 1)
                pool.tensor_tensor(cT[:, LO, g], cn[:], cT[:, HI, g].bitcast(F32), ALU.subtract).then_inc(ctx_lo, 1)

            def late(b, i):
                if i == 4:
                    spread_group(b, G - 1)
                if i == 8:
                    rest_of_group(b, G - 1)

            def step(b, before):
                if before is not None:
                    late(before, 4)
                    late(before, 8)
                for g in range(G - 1):
                    spread_group(b, g)
                    rest_of_group(b, g)
                wait(pool, x_in, 16 * b + 16)
                for t in range(T):
                    pool.tensor_tensor(xt[:, t, :], xt[:, t, :], brow[:], ALU.add).then_inc(with_bias, 1)

            pool.memset(ones[:], 1.0).then_inc(ones_set, 1)
            pool.wait_ge(ones_set, 1)
            pool.wait_ge(w_in, 32)
            over_sequences(pool, step, late)

        @block.scalar
        def _(act):
            def end_group(b, g, i):
                if i == SCALE_AT:
                    wait(act, scale_turned, b * G + g + 1)
                    wait(act, ctx_done, b * G + g)
                    act.activation(scale[:], scale_bank, ACT.Copy).then_inc(scale_done, 1)
                if i == CUT_AT and g > 0:
                    round_ctx(b, g)

            def round_ctx(b, g):
                wait(act, ctx_done, b * G + g + 1)
                if g == 0:
                    wait(act, out_made, b * T)
                act.activation(cT[:, HI, g], cn[:], ACT.Copy).then_inc(ctx_hi, 1)

            def take(b, n):
                h, t = divmod(n, T)
                g, j = divmod(h, GH)
                if n % (GH * T) == 0:
                    wait(act, ctx_made, b * G + g - 1)
                act.wait_ge(turned, b * TILES + n + 1)
                act.activation(pT[:, g % 2, j, :, t * P:(t + 1) * P],
                               turn_bank(n).rearrange("p (k q) -> p k q", k=T), ACT.Copy).then_inc(taken, 1)

            def late(b, i):
                if i < TAKE_LAG:
                    take(b, TILES - TAKE_LAG + i)
                if i < GH * T:
                    end_group(b, G - 1, i)

            def step(b, before):
                for i in range(TILES):
                    h, t = divmod(i, T)
                    g, j = divmod(h, GH)
                    if t == 0 and j == 0:
                        wait(act, inv_done, b * G + g - 1)
                    act.wait_ge(added, b * TILES + i + 1)
                    act.activation(tile[:, i % RING], tile[:, i % RING], ACT.Exp, scale=-1.0,
                                   bias=least[:, i % RING:i % RING + 1],
                                   accum_out=rowsum[:, g % 2, j, t:t + 1]).then_inc(probs, 1)
                    if before is not None:
                        late(before, i)
                    if i >= TAKE_LAG:
                        take(b, i - TAKE_LAG)
                    if g > 0:
                        end_group(b, g - 1, i % (GH * T))
                    if i == CUT0_AT:
                        round_ctx(b, 0)

            act.wait_ge(w_in, 32)
            act.activation(w[:, HI], staged, ACT.Copy).then_inc(w_hi, 1)
            act.wait_ge(w_lo, 1)
            over_sequences(act, step, late)

        @block.vector
        def _(dve):

            def add(b, n):
                t = n % T
                dve.tensor_tensor_reduce(out=tile[:, n % RING], in0=tile[:, n % RING], in1=away[:, t, :],
                                         scale=1.0, scalar=3.0e38, op0=ALU.add, op1=ALU.min,
                                         accum_out=least[:, n % RING:n % RING + 1]).then_inc(added, 1)

            def end_group(b, g, i):
                if i == INV_AT:
                    wait(dve, probs, b * TILES + (g + 1) * GH * T)
                    wait(dve, spread_done, (b * G + g) * T)
                    dve.reciprocal(inv[:], rowsum[:, g % 2]).then_inc(inv_done, 1)
                if i == CTX_AT:
                    wait(dve, scale_done, b * G + g + 1)
                    wait(dve, ctx_made, b * G + g + 1)
                    wait(dve, ctx_lo, b * G + g)
                    dve.tensor_tensor(cn[:], ctx_bank, scale[:], ALU.mult).then_inc(ctx_done, 1)

            def out_tile(b, t, bank):
                wait(dve, with_bias, b * T + t + 1)
                wait(dve, stored[t % 2], 16 * (b * (T // 2) + t // 2))
                wait(dve, out_made, b * T + t + 1)
                dve.tensor_tensor(xo[:, t % 2], bank, xt[:, t, :], ALU.add).then_inc(out_ready, 1)

            def late(b, i):
                if i < GH * T:
                    end_group(b, G - 1, i)
                if i in OUT_TAKE_AT:
                    t = OUT_TAKE_AT.index(i)
                    out_tile(b, t, out_bank(t))

            def last_adds(b):
                hold(dve, masked, b * TILES + TILES, held[:, 0:1])
                for n in range(TILES - ADD_LAG, TILES):
                    add(b, n)

            def make_away(b, t):
                dve.wait_ge(mask_in[t], 16 * b + 16)
                dve.tensor_scalar(away[:, t, :], msk[:, t, :], -10000.0, 10000.0, ALU.mult, ALU.add)\
                   .then_inc(away_done, 1)

            def step(b, before):
                new_mask = per_seq_mask or before is None
                for i in range(TILES):
                    if new_mask and i < T:
                        make_away(b, i)
                    wait(dve, turned, b * TILES + i - RING + 1)
                    wait(dve, scores, b * TILES + i + 1)
                    wait(dve, masked, b * TILES + i - ADD_LAG + 1)
                    if new_mask and ADD_LAG <= i < T + ADD_LAG:
                        dve.wait_ge(away_done, b * T + i - ADD_LAG + 1)
                    dve.scalar_tensor_tensor(tile[:, i % RING], score_bank(i), -float(HD) ** -0.5, msk[:, i % T, :],
                                             ALU.mult, ALU.mult).then_inc(masked, 1)
                    if i >= ADD_LAG:
                        add(b, i - ADD_LAG)
                    elif before is not None:
                        add(before, TILES + i - ADD_LAG)
                    if before is not None:
                        late(before, i)
                    if i >= GH * T:
                        end_group(b, i // (GH * T) - 1, i % (GH * T))

            dve.wait_ge(w_hi, 1)
            dve.tensor_tensor(w[:, LO], staged, w[:, HI].bitcast(F32), ALU.subtract).then_inc(w_lo, 1)
            step(0, None)
            with dve.Fori(1, B) as b:
                step(b, b - 1)
            last_adds(B - 1)
            for i in range(GH * T):
                end_group(B - 1, G - 1, i)
            for t in range(T):
                out_tile(B - 1, t, last_bank(t))

        @block.tensor
        def _(pe):
            def turn(b, n):
                wait(pe, taken, b * TILES + n - TURN_BANKS + 1)
                wait(pe, probs, b * TILES + n + 1)
                for k in range(T):
                    mm = pe.transpose(turn_bank(n)[:, k * P:(k + 1) * P], tile[:, n % RING, k * P:(k + 1) * P], ident[:])
                mm.then_inc(turned, 1)

            def end_group(b, g, i):
                if i == SCALE_AT:
                    wait(pe, spread_done, (b * G + g + 1) * T)
                    if g < 2:
                        wait(pe, out_ready, (b - 1) * T + (1, 3)[g])
                    for t in range(T):
                        mm = pe.transpose(scale_bank[:, t * P:(t + 1) * P],
                                          spread[:, t].rearrange("p j d -> p (j d)"), ident[:])
                    mm.then_inc(scale_turned, 1)
                if PV_AT <= i < PV_AT + T:
                    k = i - PV_AT
                    if k == 0:
                        if g == 0:
                            wait(pe, v_in, 16 * b + 16)
                        wait(pe, ctx_done, b * G + g)
                        if g < 2:
                            wait(pe, out_ready, (b - 1) * T + (2, 4)[g])
                        wait(pe, taken, b * TILES + (g + 1) * GH * T)
                    for j in range(GH):
                        h = g * GH + j
                        mm = pe.matmul(ctx_bank[j * HD:(j + 1) * HD, :], v[:, k, h * HD:(h + 1) * HD],
                                       pT[:, g % 2, j, k, :], start=(k == 0), stop=(k == T - 1))
                    if k == T - 1:
                        mm.then_inc(ctx_made, 1)

            def output_passes(bank, t, passes):
                for c, a, m in passes:
                    mm = pe.matmul(bank, cT[:, a, c, t * P:(t + 1) * P], w[:, m, c, :],
                                   start=((c, a, m) == OUT_PASSES[0]), stop=((c, a, m) == OUT_PASSES[-1]))
                return mm

            def out_tile(b, t, piece):
                if piece == 0:
                    wait(pe, ctx_lo, b * G + G)
                    wait(pe, (scale_done, ctx_done)[t % 2], b * G + G + (t >= 2))
                    if t >= 2:
                        wait(pe, out_ready, b * T + t - 1)
                count = len(OUT_PASSES) // OUT_STEPS
                mm = output_passes(out_bank(t), t, OUT_PASSES[piece * count:(piece + 1) * count])
                if piece == OUT_STEPS - 1:
                    mm.then_inc(out_made, 1)

            def finish(b):
                early, end = OUT_PASSES[:-3], OUT_PASSES[-3:]
                for n in range(TILES - LAG, TILES):
                    turn(b, n)
                pe.wait_ge(ctx_lo, b * G + G - 1)
                pe.wait_ge(masked, b * TILES + TILES)
                for t in range(BANKS):
                    output_passes(last_bank(t), t, early)
                for i in range(GH * T):
                    end_group(b, G - 1, i)
                pe.wait_ge(taken, b * TILES + TILES)
                for t in range(BANKS, T):
                    output_passes(last_bank(t), t, early)
                pe.wait_ge(ctx_lo, b * G + G)
                for t in range(T):
                    output_passes(last_bank(t), t, end).then_inc(out_made, 1)

            def late(b, i):
                if i < LAG:
                    turn(b, TILES - LAG + i)
                if i < GH * T:
                    end_group(b, G - 1, i)
                for t in range(T):
                    if OUT_AT[t] <= i < OUT_AT[t] + OUT_STEPS:
                        out_tile(b, t, i - OUT_AT[t])

            def step(b, before):
                for i in range(TILES):
                    h, t = divmod(i, T)
                    s = h % SLOTS
                    if t == 0:
                        use = b * (NH // SLOTS) + h // SLOTS + 1
                        pe.wait_ge(head_in[s], 64 * use)
                    wait(pe, masked, b * TILES + i - BANKS + 1)
                    pe.matmul(score_bank(i), qs[:, s, t * P:(t + 1) * P], ks[:, s, :], start=True, stop=True)\
                      .then_inc(scores, 1)
                    if i >= LAG:
                        turn(b, i - LAG)
                    if before is not None:
                        late(before, i)
                    if i >= GH * T:
                        end_group(b, i // (GH * T) - 1, i % (GH * T))

            step(0, None)
            with pe.Fori(1, B) as b:
                step(b, b - 1)
            finish(B - 1)

        work.close()
        pl.clear_sems()


def mlp_phase(nc, name, ps, ident, x_in, x, norm, w1, b1, w2, b2, x_out):
    STATS = 2 * T + 1
    PAIRS = M // 2
    with ExitStack() as ctx, ExitStack() as work:
        pl = Place(nc, ctx, name)
        w1s = pl.sb("w1s", [P, 2, C, FF], F32R)
        w2s = pl.sb("w2s", [P, 2, M, H], F32R)
        staged = pl.sb("staged", [P, 2, 2 * H])
        xt = pl.sb("xt", [P, T, H])
        xb = pl.sb("xb", [P, T, H])
        xh = pl.sb("xh", [P, T, H])
        full = pl.sb("full", [P, C, S])
        stats = pl.sb("stats", [P, T, 6])
        mv = pl.sb("mv", [P, T, 2])
        std = pl.sb("std", [P, T])
        rstd = pl.sb("rstd", [P, T])
        eps = pl.sb("eps", [P, 1])
        held = pl.sb("held", [P, 1])
        ln_s = pl.sb("ln_s", [P, C])
        ln_b = pl.sb("ln_b", [P, C])
        b1c = pl.sb("b1c", [P, M])
        brow = pl.sb("brow", [P, H])
        xT = pl.sb("xT", [P, 2, C, S], F32R)
        gel = pl.sb("gel", [P, 2, S])
        hT = pl.sb("hT", [P, 2, 2, S], F32R)
        xo = pl.sb("xo", [P, 2, H])

        par_in = pl.sem("par_in")
        staged_in = [pl.sem(f"staged_in{i}") for i in range(2)]
        w_hi, w_lo = pl.sem("w_hi"), pl.sem("w_lo")
        eps_set, stat, std_done = (pl.sem(n) for n in ("eps_set", "stat", "std_done"))
        normed, turned, full_done, hi_done, cut = (pl.sem(n) for n in ("normed", "turned", "full_done", "hi_done", "cut"))
        chunk_free = pl.sem("chunk_free")
        hid_made = pl.sem("hid_made")
        gel_done = pl.sem("gel_done")
        gel_hi = pl.sem("gel_hi")
        gel_cut = pl.sem("gel_cut")
        hid_used = pl.sem("hid_used")
        tile_made = pl.sem("tile_made")
        with_bias = pl.sem("with_bias")
        out_ready = pl.sem("out_ready")
        stored = [pl.sem(f"stored{i}") for i in range(2)]

        turn_bank = lambda n: ps[:, n % 2, :]
        hid_bank = lambda n: ps[:, 2 + n % 2, :]
        out_bank = lambda t: ps[:, 4 + t, :]
        w1_piece = lambda j, part: w1s[:, part, :, j * 2 * P:(j + 1) * 2 * P]
        w2_piece = lambda j, part: w2s[:, part, 2 * j:2 * j + 2, :].rearrange("p m n -> p (m n)")
        piece = lambda n, part: (w1_piece, w2_piece)[n % 2](n // 2, part)
        staged_piece = lambda n: (staged[:, 0].rearrange("p (c n) -> p c n", c=C), staged[:, 1])[n % 2]
        PREPARE_AT = 2
        TURN_AT = 6
        block = work.enter_context(nc.Block())

        def over_ahead(eng, step):
            step(0, 1)
            with eng.Fori(1, B - 1) as b:
                step(b, b + 1)
            step(B - 1, None)

        @block.sync
        def _(sp):
            for to, src in ((ln_s[:], norm[0]), (ln_b[:], norm[1]), (b1c[:], b1), (brow[:], row(b2, H))):
                sp.dma_start(to, src).then_inc(par_in, 16)
            for n in range(2 * PAIRS):
                wait(sp, w_lo, n - 1)
                j = n // 2
                if n % 2 == 0:
                    sp.dma_start(staged_piece(n), chunks(w1[:, j * 2 * P:(j + 1) * 2 * P])).then_inc(staged_in[0], 16)
                else:
                    sp.dma_start(staged[:, 1].rearrange("p (m n) -> p m n", n=H), chunks(w2[j * 2 * P:(j + 1) * 2 * P, :]))\
                      .then_inc(staged_in[1], 16)

            def step(b):
                for t in range(T):
                    sp.wait_ge(out_ready, b * T + t + 1)
                    sp.dma_start(x_out[b, t * P:(t + 1) * P, :], xo[:, t % 2, :]).then_inc(stored[t % 2], 16)

            over_batch(sp, step)
            for s in stored:
                sp.wait_ge(s, 16 * B * T // 2)

        @block.gpsimd
        def _(pool):
            def add_bias(b):
                wait(pool, out_ready, b * T)
                for t in range(T):
                    pool.tensor_tensor(xb[:, t, :], xt[:, t, :], brow[:], ALU.add).then_inc(with_bias, 1)

            def step(b):
                add_bias(b)
                pool.wait_ge(normed, b * T + T)
                pool.wait_ge(with_bias, b * T + T)
                pool.dma_start(xt[:], tiles(x, b + 1)).then_inc(x_in, 16)
                pool.wait_ge(x_in, 16 * b + 32)

            pool.dma_start(xt[:], tiles(x, 0)).then_inc(x_in, 16)
            pool.wait_ge(par_in, 64)
            pool.wait_ge(x_in, 16)
            step(0)
            with pool.Fori(1, B - 1) as b:
                step(b)
            add_bias(B - 1)

        @block.scalar
        def _(act):
            def root(b):
                act.wait_ge(stat, b * STATS + 2 * T)
                act.activation(std[:], mv[:, :, 1], ACT.Sqrt, bias=eps[:, 0:1]).then_inc(std_done, 1)

            def take(b, c):
                wait(act, cut, (b - 1) * C + c + 1)
                act.wait_ge(turned, b * C + c + 1)
                act.activation(full[:, c], turn_bank(c), ACT.Identity, bias=ln_b[:, c:c + 1],
                               scale=ln_s[:, c:c + 1]).then_inc(full_done, 1)

            def round_chunk(b, c):
                act.wait_ge(full_done, b * C + c + 1)
                if c < C - 1:
                    wait(act, chunk_free, (b - 1) * (C - 1) + c + 1)
                else:
                    wait(act, hid_made, b * M)
                act.activation(xT[:, HI, c], full[:, c], ACT.Copy).then_inc(hi_done, 1)

            def round_weights(n):
                act.wait_ge(staged_in[n % 2], 16 * (n // 2 + 1))
                act.activation(piece(n, HI), staged_piece(n), ACT.Copy).then_inc(w_hi, 1)

            def step(b, ahead):
                for m in range(M):
                    if isinstance(b, int) and b == 0:
                        if m + 4 < 2 * PAIRS:
                            round_weights(m + 4)
                    if m == M - 1 and ahead is not None:
                        for c in range(C):
                            round_chunk(ahead, c)
                    n = b * M + m
                    wait(act, gel_cut, n - 1)
                    act.wait_ge(hid_made, n + 1)
                    act.activation(gel[:, m % 2], hid_bank(m), ACT.Gelu_apprx_tanh, bias=b1c[:, m:m + 1])\
                       .then_inc(gel_done, 1)
                    if ahead is not None:
                        if m == PREPARE_AT:
                            root(ahead)
                        if TURN_AT < m <= TURN_AT + C:
                            take(ahead, m - TURN_AT - 1)

            act.wait_ge(par_in, 64)
            act.wait_ge(eps_set, 1)
            root(0)
            for n in range(2):
                round_weights(n)
            for c in range(C):
                take(0, c)
            for c in range(C):
                round_chunk(0, c)
            for n in range(2, 4):
                round_weights(n)
            over_ahead(act, step)

        @block.vector
        def _(dve):
            def statistics(b):
                dve.wait_ge(x_in, 16 * b + 16)
                for t in range(T):
                    dve.bn_stats(stats[:, t, :], xt[:, t, :]).then_inc(stat, 1)
                hold(dve, stat, b * STATS + T, held[:, 0:1])
                for t in range(T):
                    dve.bn_aggr(mv[:, t, :], stats[:, t, :]).then_inc(stat, 1)

            def normalise(b):
                dve.wait_ge(std_done, b + 1)
                dve.reciprocal(rstd[:], std[:]).then_inc(stat, 1)
                dve.wait_ge(stat, b * STATS + STATS)
                wait(dve, turned, b * C)
                for t in range(T):
                    dve.tensor_scalar(xh[:, t, :], xt[:, t, :], mv[:, t, 0:1], rstd[:, t:t + 1],
                                      ALU.subtract, ALU.mult).then_inc(normed, 1)

            def rest_of_chunk(b, c):
                dve.wait_ge(hi_done, b * C + c + 1)
                dve.tensor_tensor(xT[:, LO, c], full[:, c], xT[:, HI, c].bitcast(F32), ALU.subtract)\
                   .then_inc(cut, 1)

            def rest_of_weights(n):
                dve.wait_ge(w_hi, n + 1)
                dve.tensor_tensor(piece(n, LO), staged_piece(n), piece(n, HI).bitcast(F32), ALU.subtract)\
                   .then_inc(w_lo, 1)

            def step(b, ahead):
                for m in range(M):
                    if isinstance(b, int) and b == 0:
                        if m + 4 < 2 * PAIRS:
                            rest_of_weights(m + 4)
                    if m == M - 1 and ahead is not None:
                        for c in range(C):
                            rest_of_chunk(ahead, c)
                    n = b * M + m
                    if m >= 2:
                        dve.wait_ge(hid_used, b * (M - 1) + m - 1)
                    dve.wait_ge(gel_done, n + 1)
                    dve.tensor_copy(hT[:, m % 2, HI], gel[:, m % 2]).then_inc(gel_hi, 1)
                    dve.wait_ge(gel_hi, n + 1)
                    dve.tensor_tensor(hT[:, m % 2, LO], gel[:, m % 2], hT[:, m % 2, HI].bitcast(F32), ALU.subtract)\
                       .then_inc(gel_cut, 1)
                    if ahead is not None:
                        if m == PREPARE_AT:
                            statistics(ahead)
                        if m == PREPARE_AT + 1:
                            normalise(ahead)
                dve.wait_ge(with_bias, b * T + T)
                for t in range(T):
                    wait(dve, stored[t % 2], 16 * (b * (T // 2) + t // 2))
                    dve.wait_ge(tile_made, b * T + t + 1)
                    dve.tensor_tensor(xo[:, t % 2], out_bank(t), xb[:, t, :], ALU.add).then_inc(out_ready, 1)

            dve.memset(eps[:], EPS).then_inc(eps_set, 1)
            statistics(0)
            normalise(0)
            for n in range(2):
                rest_of_weights(n)
            for c in range(C):
                rest_of_chunk(0, c)
            for n in range(2, 4):
                rest_of_weights(n)
            over_ahead(dve, step)

        @block.tensor
        def _(pe):
            def turn(b, c):
                if c < 2:
                    wait(pe, full_done, (b - 1) * C + C - 1 + c)
                else:
                    pe.wait_ge(full_done, b * C + c - 1)
                if c == 0:
                    pe.wait_ge(normed, b * T + T)
                for t in range(T):
                    mm = pe.transpose(turn_bank(c)[:, t * P:(t + 1) * P], xh[:, t, c * P:(c + 1) * P], ident[:])
                mm.then_inc(turned, 1)

            def step(b, ahead):
                for m in range(M + 2):
                    if m < M:
                        if isinstance(b, int) and b == 0 and m % 2 == 0:
                            pe.wait_ge(w_lo, m + 1)
                        wait(pe, gel_done, b * M + m - 1)
                        for c in range(C):
                            if m == 0:
                                pe.wait_ge(cut, b * C + c + 1)
                            for n, (a, r) in enumerate(PASSES):
                                mm = pe.matmul(hid_bank(m), w1s[:, a, c, m * P:(m + 1) * P], xT[:, r, c, :],
                                               start=(c == 0 and n == 0), stop=(c == C - 1 and n == 2))
                            if c == C - 1:
                                mm.then_inc(hid_made, 1)
                            elif m == M - 1:
                                mm.then_inc(chunk_free, 1)
                    k = m - 2
                    if k >= 0:
                        if isinstance(b, int) and b == 0 and k % 2 == 0:
                            pe.wait_ge(w_lo, k + 2)
                        pe.wait_ge(gel_cut, b * M + k + 1)
                        for t in range(T):
                            if k == 0:
                                wait(pe, out_ready, (b - 1) * T + t + 1)
                            for n, (a, r) in enumerate(PASSES):
                                mm = pe.matmul(out_bank(t), hT[:, k % 2, a, t * P:(t + 1) * P], w2s[:, r, k, :],
                                               start=(k == 0 and n == 0), stop=(k == M - 1 and n == 2))
                            if k == M - 1:
                                mm.then_inc(tile_made, 1)
                        if k < M - 1:
                            mm.then_inc(hid_used, 1)
                    if ahead is not None and TURN_AT <= m < TURN_AT + C:
                        turn(ahead, m - TURN_AT)

            for c in range(C):
                turn(0, c)
            over_ahead(pe, step)

        work.close()
        pl.clear_sems()


def last_phase(nc, name, ps, ident, e_in, x, enc, w_q, w_k, w_v, w_o, alpha, x_out):
    with ExitStack() as ctx, ExitStack() as work:
        pl = Place(nc, ctx, name)
        wq, wk, wv, wo = (pl.sb(n, [P, C, H]) for n in ("wq", "wk", "wv", "wo"))
        woT = pl.sb("woT", [P, C, H])
        kq = pl.sb("kq", [P, 2, C, H], F32R)
        vo = pl.sb("vo", [P, 2, C, H], F32R)
        al = pl.sb("al", [P, 1])
        xt = pl.sb("xt", [P, 2, T, H])
        kept = pl.sb("kept", [P, T, H])
        xT = pl.sb("xT", [P, 2, 2, C, S], F32R)
        gT = pl.sb("gT", [P, 2, C, S], F32R)
        u = pl.sb("u", [P, 2, T, H], F32R)
        sc = pl.sb("sc", [P, 4, S])
        least = pl.sb("least", [P, T])
        rowsum = pl.sb("rowsum", [P, T])
        inv = pl.sb("inv", [P, T])
        by = pl.sb("by", [P, T])
        pT = pl.sb("pT", [P, 2, 2, T, P], F32R)
        xo = pl.sb("xo", [P, 2, H])

        kq_in, vo_in = pl.sem("kq_in"), pl.sem("vo_in")
        pre_made = pl.sem("pre_made")
        pre_hi = pl.sem("pre_hi")
        pre_done = pl.sem("pre_done")
        x_in = pl.sem("x_loaded")
        turned = pl.sem("turned")
        turn_hi = pl.sem("turn_hi")
        cut = pl.sem("cut")
        made = pl.sem("made")
        made_hi = pl.sem("made_hi")
        made_cut = pl.sem("made_cut")
        x_kept = pl.sem("x_kept")
        scores = pl.sem("scores")
        least_done = pl.sem("least_done")
        probs = pl.sem("probs")
        inv_done, by_done = pl.sem("inv_done"), pl.sem("by_done")
        p_turned, p_hi, p_cut = pl.sem("p_turned"), pl.sem("p_hi"), pl.sem("p_cut")
        delta = pl.sem("delta")
        out_ready = pl.sem("out_ready")
        stored = [pl.sem(f"stored{i}") for i in range(2)]

        N = 2 * C
        KQ, WOT, VO = range(3)
        p_bank = lambda t: ps[:, t % 2, :]
        turn_bank = lambda n: ps[:, 2 + n % 2, :]
        score_bank = lambda t: ps[:, 2 + t % 2, :]
        bank4 = lambda n: ps[:, 4 + n % 4, :]
        block = work.enter_context(nc.Block())

        def over_ahead(eng, step):
            step(0, 1)
            with eng.Fori(1, B - 1) as b:
                step(b, b + 1)
            step(B - 1, None)

        @block.sync
        def _(sp):
            sp.dma_start(wk[:], chunks(w_k)).then_inc(kq_in, 16)
            sp.dma_start(wq[:], chunks(w_q)).then_inc(kq_in, 16)
            sp.dma_start(xt[:, 0], tiles(x, 0)).then_inc(x_in, 16)
            sp.dma_start(wo[:], chunks(w_o)).then_inc(vo_in, 16)
            sp.dma_start(wv[:], chunks(w_v)).then_inc(vo_in, 16)
            sp.dma_start(al[:], alpha.rearrange("(a n) -> a n", a=1).broadcast_to([P, 1])).then_inc(vo_in, 16)

            def step(b, ahead):
                if ahead is not None:
                    sp.wait_ge(turned, ahead * N)
                    sp.wait_ge(x_kept, ahead)
                    sp.dma_start(xt[:, 0], tiles(x, ahead)).then_inc(x_in, 16)
                for t in range(T):
                    sp.wait_ge(out_ready, b * T + t + 1)
                    sp.dma_start(x_out[b, t * P:(t + 1) * P, :], xo[:, t % 2, :]).then_inc(stored[t % 2], 16)

            over_ahead(sp, step)
            for s in stored:
                sp.wait_ge(s, 16 * B * T // 2)

        @block.gpsimd
        def _(pool):
            pool.dma_start(xt[:, 1], tiles(enc, 0)).then_inc(e_in, 16)
            with pool.Fori(1, B) as b:
                pool.wait_ge(turned, b * N - C)
                pool.dma_start(xt[:, 1], tiles(enc, b)).then_inc(e_in, 16)

        @block.scalar
        def _(act):
            def round_turned(b, n):
                act.wait_ge(turned, b * N + n + 1)
                if n == 0:
                    wait(act, made, b * N)
                if n == C:
                    wait(act, scores, b * T)
                act.activation(xT[:, 1 - n // C, HI, n % C], turn_bank(n), ACT.Copy).then_inc(turn_hi, 1)

            def round_made(b, n):
                act.wait_ge(made, b * N + n + 1)
                if n == 0:
                    wait(act, scores, b * T)
                if n == C:
                    wait(act, delta, b * T)
                to = gT[:, HI, n, :] if n < C else u[:, HI, n - C, :]
                act.activation(to, bank4(n), ACT.Copy).then_inc(made_hi, 1)

            def keep(b):
                act.wait_ge(x_in, 16 * b + 16)
                wait(act, out_ready, b * T)
                act.activation(kept[:], xt[:, 0], ACT.Copy).then_inc(x_kept, 1)

            def round_probs(b, t):
                wait(act, delta, b * T + t - 1)
                act.wait_ge(p_turned, b * T + t + 1)
                act.activation(pT[:, t % 2, HI].rearrange("p k q -> p (k q)"), p_bank(t), ACT.Copy).then_inc(p_hi, 1)

            def prepare(b):
                for n in range(N):
                    round_made(b, n)
                keep(b)

            def step(b, ahead):
                for t in range(T):
                    act.wait_ge(least_done, b * T + t + 1)
                    if t == 0:
                        wait(act, inv_done, b)
                    act.activation(sc[:, t], sc[:, t], ACT.Exp, scale=-1.0, bias=least[:, t:t + 1],
                                   accum_out=rowsum[:, t:t + 1]).then_inc(probs, 1)
                for t in range(T):
                    round_probs(b, t)
                    if ahead is not None:
                        round_turned(ahead, t)
                if ahead is not None:
                    for c in range(C):
                        round_turned(ahead, C + c)
                    prepare(ahead)

            for n in range(C):
                round_turned(0, n)
            for n in range(3 * C):
                i, c = divmod(n, C)
                if n == C:
                    for k in range(C):
                        round_turned(0, C + k)
                act.wait_ge(pre_made, n + 1)
                to = woT[:, c, :] if i == WOT else (kq if i == KQ else vo)[:, HI, c, :]
                act.activation(to, bank4(n), ACT.Copy).then_inc(pre_hi, 1)
            prepare(0)
            over_ahead(act, step)

        @block.vector
        def _(dve):
            def rest_of_turned(b, n):
                which = 1 - n // C
                dve.wait_ge(turn_hi, b * N + n + 1)
                dve.tensor_tensor(xT[:, which, LO, n % C], turn_bank(n), xT[:, which, HI, n % C].bitcast(F32),
                                  ALU.subtract).then_inc(cut, 1)

            def rest_of_made(b, n):
                dve.wait_ge(made_hi, b * N + n + 1)
                to = gT[:, :, n, :] if n < C else u[:, :, n - C, :]
                dve.tensor_tensor(to[:, LO], bank4(n), to[:, HI].bitcast(F32), ALU.subtract).then_inc(made_cut, 1)

            def rest_of_probs(b, t):
                dve.wait_ge(p_hi, b * T + t + 1)
                dve.tensor_tensor(pT[:, t % 2, LO].rearrange("p k q -> p (k q)"), p_bank(t),
                                  pT[:, t % 2, HI].rearrange("p k q -> p (k q)").bitcast(F32),
                                  ALU.subtract).then_inc(p_cut, 1)

            def output(b, t):
                if t == 0:
                    dve.wait_ge(by_done, b + 1)
                    dve.wait_ge(x_kept, b + 1)
                wait(dve, stored[t % 2], 16 * (b * (T // 2) + t // 2))
                dve.wait_ge(delta, b * T + t + 1)
                dve.scalar_tensor_tensor(xo[:, t % 2], bank4(t), by[:, t:t + 1], kept[:, t, :],
                                         ALU.mult, ALU.add).then_inc(out_ready, 1)

            def step(b, ahead):
                for t in range(T):
                    dve.wait_ge(scores, b * T + t + 1)
                    wait(dve, p_turned, (b - 1) * T + t + 1)
                    dve.tensor_scalar(sc[:, t], score_bank(t), -float(H) ** -0.5, None, ALU.mult, ALU.min,
                                      accum_out=least[:, t:t + 1]).then_inc(least_done, 1)
                for t in range(T):
                    rest_of_probs(b, t)
                    if ahead is not None:
                        rest_of_turned(ahead, t)
                    if t == 1:
                        dve.wait_ge(probs, b * T + T)
                        dve.reciprocal(inv[:], rowsum[:]).then_inc(inv_done, 1)
                        dve.wait_ge(inv_done, b + 1)
                        dve.tensor_scalar(by[:], inv[:], al[:, 0:1], None, ALU.mult).then_inc(by_done, 1)
                    if t >= 2:
                        output(b, t - 2)
                for t in range(2, T):
                    if ahead is not None:
                        rest_of_turned(ahead, C + t - 2)
                    output(b, t)
                if ahead is not None:
                    for n in range(C + T - 2, N):
                        rest_of_turned(ahead, n)
                    for n in range(N):
                        rest_of_made(ahead, n)

            for n in range(C):
                rest_of_turned(0, n)
            dve.wait_ge(vo_in, 48)
            for n in range(2 * C):
                w, c = (kq, vo)[n // C], n % C
                if n == C:
                    for k in range(C):
                        rest_of_turned(0, C + k)
                dve.wait_ge(pre_hi, n + 1 if n < C else n + C + 1)
                dve.tensor_tensor(w[:, LO, c, :], bank4(n), w[:, HI, c, :].bitcast(F32), ALU.subtract)\
                   .then_inc(pre_done, 1)
            for n in range(N):
                rest_of_made(0, n)
            over_ahead(dve, step)

        @block.tensor
        def _(pe):
            def turn(b, n):
                which, c = 1 - n // C, n % C
                if n == 0:
                    pe.wait_ge(e_in, 16 * b + 16)
                if n == C:
                    pe.wait_ge(x_in, 16 * b + 16)
                if n < 2:
                    wait(pe, least_done, b * T + n - 1)
                else:
                    pe.wait_ge(cut, b * N + n - 1)
                for t in range(T):
                    mm = pe.transpose(turn_bank(n)[:, t * P:(t + 1) * P], xt[:, which, t, c * P:(c + 1) * P], ident[:])
                mm.then_inc(turned, 1)

            def product(bank, stationary, moving):
                n = 0
                for c in range(C):
                    for a, r in PASSES:
                        mm = pe.matmul(bank, stationary(a, c), moving(r, c), start=(n == 0), stop=(n == 3 * C - 1))
                        n += 1
                return mm

            def make(b, n):
                if n == 0:
                    pe.wait_ge(cut, b * N + C)
                if n >= C:
                    pe.wait_ge(made_cut, b * N + n - C + 1)
                elif isinstance(b, int) and b == 0:
                    pe.wait_ge(pre_done, C + n + 1)
                else:
                    pe.wait_ge(out_ready, (b - 1) * T + n + 1)
                part = slice((n % C) * P, (n % C + 1) * P)
                if n < C:
                    mm = product(bank4(n), lambda a, c: kq[:, a, c, part], lambda r, c: xT[:, 1, r, c, :])
                else:
                    mm = product(bank4(n), lambda a, c: xT[:, 1, a, c, part], lambda r, c: vo[:, r, c, :])
                mm.then_inc(made, 1)

            def turn_probs(b, t):
                pe.wait_ge(probs, b * T + t + 1)
                wait(pe, p_cut, b * T + t - 1)
                for k in range(T):
                    mm = pe.transpose(p_bank(t)[:, k * P:(k + 1) * P], sc[:, t, k * P:(k + 1) * P], ident[:])
                mm.then_inc(p_turned, 1)

            def weigh(b, t):
                pe.wait_ge(made_cut, b * N + C + T)
                pe.wait_ge(p_cut, b * T + t + 1)
                product(bank4(t), lambda a, c: pT[:, t % 2, a, c, :], lambda r, c: u[:, r, c, :]).then_inc(delta, 1)

            def step(b, ahead):
                pe.wait_ge(cut, b * N + N)
                pe.wait_ge(made_cut, b * N + C)
                for t in range(T):
                    if t >= 2:
                        pe.wait_ge(least_done, b * T + t - 1)
                    part = slice(t * P, (t + 1) * P)
                    product(score_bank(t), lambda a, c: xT[:, 0, a, c, part], lambda r, c: gT[:, r, c, :])\
                        .then_inc(scores, 1)
                for t in range(T + 2):
                    if t < T:
                        turn_probs(b, t)
                        if ahead is not None:
                            turn(ahead, t)
                    if 1 <= t <= T:
                        weigh(b, t - 1)
                    if ahead is not None and t >= T - 1:
                        turn(ahead, C + t - T + 1)
                if ahead is not None:
                    turn(ahead, N - 1)
                    for n in range(N):
                        make(ahead, n)

            for n in range(C):
                turn(0, n)
            for n in range(3 * C):
                i, c = divmod(n, C)
                if n == 0:
                    pe.wait_ge(kq_in, 32)
                if n == C:
                    for k in range(C):
                        turn(0, C + k)
                    pe.wait_ge(vo_in, 48)
                if i == WOT:
                    pe.wait_ge(pre_done, c + 1)
                if i == VO:
                    pe.wait_ge(pre_hi, 2 * C)
                for k in range(C):
                    part = slice(c * P, (c + 1) * P)
                    if i == WOT:
                        mm = pe.transpose(bank4(n)[:, k * P:(k + 1) * P], wo[:, k, part], ident[:])
                    elif i == KQ:
                        mm = pe.matmul(bank4(n), wk[:, k, part], wq[:, k, :], start=(k == 0), stop=(k == C - 1))
                    else:
                        mm = pe.matmul(bank4(n), wv[:, k, part], woT[:, k, :], start=(k == 0), stop=(k == C - 1))
                mm.then_inc(pre_made, 1)
            for n in range(N):
                make(0, n)
            over_ahead(pe, step)

        work.close()
        pl.clear_sems()


def layer_and_cross_attention_kernel(nc, a, out):
    with ExitStack() as ctx:
        scratch = {
            "heads": nc.dram_tensor("heads", [2, B, G, 2, P, S], F32, kind="Internal").ap(),
            "v": nc.dram_tensor("v_scratch", [B, P, T, H], F32, kind="Internal").ap(),
        }
        x1 = nc.dram_tensor("x1", [B, S, H], F32, kind="Internal").ap()
        x2 = nc.dram_tensor("x2", [B, S, H], F32, kind="Internal").ap()
        x3 = nc.dram_tensor("x3", [B, S, H], F32, kind="Internal").ap()
        ps = ctx.enter_context(nc.psum_tensor("ps", [P, 8, S], F32))
        ident = ctx.enter_context(nc.sbuf_tensor("ident", [P, P], F32))
        zeroed = ctx.enter_context(nc.semaphore("zeroed"))
        ident_set = ctx.enter_context(nc.semaphore("ident_set"))

        x_in = {n: ctx.enter_context(nc.semaphore(f"{n}_x_in")) for n in ("self_qkv", "cross_kvq", "mlp", "last")}

        with nc.Block() as block:
            @block.gpsimd
            def _(pool):
                nc.gpsimd.memset(ident[:], 0.0).then_inc(zeroed, 1)
                pool.wait_ge(zeroed, 1)
                nc.gpsimd.affine_select(out=ident[:], in_=ident[:], compare_op=ALU.not_equal, fill=1.0, base=0,
                                        pattern=[[-1, P]], channel_multiplier=1).then_inc(ident_set, 1)
                pool.wait_ge(ident_set, 1)

        cqkv, ckv = a["columns_L0_xattn_b_qkv"], a["columns_L0_xattn_b_kv"]
        col = lambda v, i: v[:, i * C:(i + 1) * C]
        wqkv, wkv = a["L0_xattn_w_qkv"], a["L0_xattn_w_kv"]
        bqkv, bkv = a["L0_xattn_b_qkv"], a["L0_xattn_b_kv"]
        cut = lambda w, i: w[:, i * H:(i + 1) * H]
        vec = lambda v, i: v[i * H:(i + 1) * H]
        project_phase(nc, "self_qkv", ps, ident, x_in["self_qkv"], [
            (a["x"], (a["columns_L0_xattn_ln1_s"], a["columns_L0_xattn_ln1_b"]),
             [(cut(wqkv, 1), col(cqkv, 1), K), (cut(wqkv, 0), col(cqkv, 0), Q), (cut(wqkv, 2), vec(bqkv, 2), None)])],
                      scratch)
        attention_phase(nc, "self_att", ps, ident, scratch, Q, K, a["mask_1x1xSxS2_fc1"], a["L0_xattn_w_ao"],
                        a["L0_xattn_b_ao"], a["x"], x1)
        project_phase(nc, "cross_kvq", ps, ident, x_in["cross_kvq"], [
            (a["ctx_2048"], None, [(cut(wkv, 0), col(ckv, 0), K), (cut(wkv, 1), vec(bkv, 1), None)]),
            (x1, (a["columns_L0_xattn_ln2_s"], a["columns_L0_xattn_ln2_b"]),
             [(a["L0_xattn_w_q"], a["columns_L0_xattn_b_q"], Q)])], scratch)
        attention_phase(nc, "cross_att", ps, ident, scratch, Q, K, a["mask_Bx1xSxS2_ff1"], a["L0_xattn_w_co"],
                        a["L0_xattn_b_co"], x1, x2)
        mlp_phase(nc, "mlp", ps, ident, x_in["mlp"], x2, (a["columns_L0_xattn_ln3_s"], a["columns_L0_xattn_ln3_b"]), a["L0_xattn_w1"],
                  a["columns_L0_xattn_b1"], a["L0_xattn_w2"], a["L0_xattn_b2"], x3)
        last_phase(nc, "last", ps, ident, x_in["last"], x3, a["ctx_2048"], a["L1_xattn_w_q"], a["L1_xattn_w_k"],
                   a["L1_xattn_w_v"], a["L1_xattn_w_o"], a["L1_xattn_alpha"], out)


_INS = ["x", "ctx_2048", "mask_1x1xSxS2_fc1", "mask_Bx1xSxS2_ff1", "L0_xattn_ln1_s", "L0_xattn_ln1_b",
        "L0_xattn_w_qkv", "L0_xattn_b_qkv", "L0_xattn_w_ao", "L0_xattn_b_ao", "L0_xattn_ln2_s", "L0_xattn_ln2_b",
        "L0_xattn_w_q", "L0_xattn_b_q", "L0_xattn_w_kv", "L0_xattn_b_kv", "L0_xattn_w_co", "L0_xattn_b_co",
        "L0_xattn_ln3_s", "L0_xattn_ln3_b", "L0_xattn_w1", "L0_xattn_b1", "L0_xattn_w2", "L0_xattn_b2",
        "L1_xattn_w_q", "L1_xattn_w_k", "L1_xattn_w_v", "L1_xattn_w_o", "L1_xattn_alpha"]

_COLUMNS = ["L0_xattn_ln1_s", "L0_xattn_ln1_b", "L0_xattn_b_qkv", "L0_xattn_ln2_s", "L0_xattn_ln2_b",
            "L0_xattn_b_q", "L0_xattn_b_kv", "L0_xattn_ln3_s", "L0_xattn_ln3_b", "L0_xattn_b1"]


def kernel(**inputs):
    import numpy as _np
    import concourse.bacc as _bacc
    from concourse import mybir as _mybir
    from concourse.bass_utils import run_bass_kernel_spmd as _run

    nc = _bacc.Bacc("TRN2", target_bir_lowering=False, num_devices=1)
    arrays, args = {}, {}
    given = {name: _np.asarray(inputs[name]).reshape(inputs[name].shape or (1,)) for name in _INS}
    given |= {f"columns_{name}": given[name].reshape(-1, P).T for name in _COLUMNS}
    for name, a in given.items():
        a = _np.ascontiguousarray(a)
        arrays[f"in_{name}"] = a
        args[name] = nc.dram_tensor(f"in_{name}", a.shape, _mybir.dt.from_np(a.dtype), kind="ExternalInput").ap()
    out = nc.dram_tensor("out_0", (B, S, H), F32, kind="ExternalOutput").ap()
    layer_and_cross_attention_kernel(nc, args, out)
    r = _run(nc, [arrays], core_ids=[0])
    return r.results[0]["out_0"]
```
